# Optimizing a Trainium2 kernel written in Bass

```python
import numpy as np
import jax
import jax.numpy as jnp

def _softmax(x, axis=-1):
    return jax.nn.softmax(x, axis=axis)

def _gelu(x):
    return jax.nn.gelu(x, approximate=True)

def _silu(x):
    return jax.nn.silu(x)

def _sigmoid(x):
    return jax.nn.sigmoid(x)

def _layernorm(x, axis=-1, eps=1e-05):
    m = jnp.mean(x, axis=axis, keepdims=True)
    v = jnp.var(x, axis=axis, keepdims=True)
    return (x - m) / jnp.sqrt(v + eps)

def _scatter_add(tgt, idx, src, axis=0):
    return tgt.at[idx].add(src)

def _segment_sum(src, seg, n):
    return jax.ops.segment_sum(src, seg, n)
kernel_name = 'mk_adaln_d1_jaxref_r4_19d30b'

def setup_inputs(seed: int=0):
    np.random.seed(seed)
    _w = jnp.asarray

    def _L0_attn_setup():
        import jax, jax.numpy as jnp
        import numpy as np
        import math
        N_HEAD = 16
        HEAD_QKV = 256
        WM_DECAY_LENGTH = 512
        WM_DECAY_RATE = 1.0
        WM_ECHOIC = 16

        def decay_weight_matrix(n):
            dl = WM_DECAY_LENGTH - WM_ECHOIC + 1
            nums = jnp.linspace(0.0, 1.0, dl)
            decay_values = 1.0 - jnp.power(nums, 1.0 / (np.e * WM_DECAY_RATE))
            decay_values = jnp.concatenate([jnp.ones(WM_ECHOIC - 1), decay_values])
            decay_values = decay_values[:n]
            idx = jnp.arange(n)[:, None] - jnp.arange(n)[None, :]
            mat = decay_values[jnp.clip(idx, 0, n - 1)]
            return jnp.tril(mat).astype(jnp.float32)
        key = jax.random.key(seed)
        k1, k2, k3 = jax.random.split(key, 3)
        B, T, C = (2, 512, 256)
        x = jax.random.normal(k1, (B, T, C), dtype=jnp.float32)
        W_attn = jax.random.normal(k2, (C, 3 * HEAD_QKV), dtype=jnp.float32) * (1.0 / math.sqrt(C))
        W_proj = jax.random.normal(k3, (HEAD_QKV, C), dtype=jnp.float32) * (1.0 / math.sqrt(HEAD_QKV))
        return {'x': x, 'W_attn': W_attn, 'W_proj': W_proj}
    _L0_attn_in = _L0_attn_setup()

    def _L0_ffn_setup():
        import jax, jax.numpy as jnp
        import numpy as np
        ALPHA = 1.0
        key = jax.random.key(seed)
        ks = jax.random.split(key, 7)
        B, S, IN, OUT = (8, 2048, 256, 256)
        RANK, DDIM, UDIM = (4, 100, 50)
        return {'hidden_states': jax.random.normal(ks[0], (B, S, IN), dtype=jnp.float32), 'W': jax.random.normal(ks[1], (OUT, IN), dtype=jnp.float32) * 0.02, 'b': jax.random.normal(ks[2], (OUT,), dtype=jnp.float32) * 0.02, 'lora_down': jax.random.normal(ks[3], (RANK, DDIM), dtype=jnp.float32) * 0.1, 'lora_up': jax.random.normal(ks[4], (UDIM, RANK), dtype=jnp.float32) * 0.1, 'down_aux': jax.random.normal(ks[5], (DDIM, IN), dtype=jnp.float32) * 0.03, 'up_aux': jax.random.normal(ks[6], (OUT, UDIM), dtype=jnp.float32) * 0.03}
    _L0_ffn_in = _L0_ffn_setup()
    _L0_c = _w((lambda *s: np.random.randn(*s).astype(np.float32) * 0.05)(1, 256))
    _L0_wmod = _w((lambda *s: np.random.randn(*s).astype(np.float32) * 0.05)(256, 6 * 256) * 256 ** (-0.5))
    _d = {'L0_attn_x': _L0_attn_in['x'], 'L0_attn_W_attn': _L0_attn_in['W_attn'], 'L0_attn_W_proj': _L0_attn_in['W_proj'], 'L0_ffn_W': _L0_ffn_in['W'], 'L0_ffn_b': _L0_ffn_in['b'], 'L0_ffn_lora_down': _L0_ffn_in['lora_down'], 'L0_ffn_lora_up': _L0_ffn_in['lora_up'], 'L0_ffn_down_aux': _L0_ffn_in['down_aux'], 'L0_ffn_up_aux': _L0_ffn_in['up_aux'], 'L0_c': _L0_c, 'L0_wmod': _L0_wmod}
    _x0 = _d['L0_attn_x']
    _d['L0_attn_x'] = jax.random.normal(jax.random.fold_in(jax.random.key(seed), 1), (1, 4096, 256), dtype=_x0.dtype)
    del _x0
    return _d

def reference(L0_attn_x, L0_attn_W_attn, L0_attn_W_proj, L0_ffn_W, L0_ffn_b, L0_ffn_lora_down, L0_ffn_lora_up, L0_ffn_down_aux, L0_ffn_up_aux, L0_c, L0_wmod):

    def _L0_attn_ref(x, W_attn, W_proj):
        import jax, jax.numpy as jnp
        import numpy as np
        import math
        N_HEAD = 16
        HEAD_QKV = 256
        WM_DECAY_LENGTH = 512
        WM_DECAY_RATE = 1.0
        WM_ECHOIC = 16

        def decay_weight_matrix(n):
            dl = WM_DECAY_LENGTH - WM_ECHOIC + 1
            nums = jnp.linspace(0.0, 1.0, dl)
            decay_values = 1.0 - jnp.power(nums, 1.0 / (np.e * WM_DECAY_RATE))
            decay_values = jnp.concatenate([jnp.ones(WM_ECHOIC - 1), decay_values])
            decay_values = decay_values[:n]
            idx = jnp.arange(n)[:, None] - jnp.arange(n)[None, :]
            mat = decay_values[jnp.clip(idx, 0, n - 1)]
            return jnp.tril(mat).astype(jnp.float32)
        B, T, C = x.shape
        hd = HEAD_QKV // N_HEAD
        qkv = x @ W_attn
        q, k, v = jnp.split(qkv, 3, axis=-1)
        q = q.reshape(B, T, N_HEAD, hd).transpose(0, 2, 1, 3)
        k = k.reshape(B, T, N_HEAD, hd).transpose(0, 2, 1, 3)
        v = v.reshape(B, T, N_HEAD, hd).transpose(0, 2, 1, 3)
        att = jnp.einsum('bhqd,bhkd->bhqk', q, k) * (1.0 / math.sqrt(hd))
        causal = jnp.tril(jnp.ones((T, T), dtype=bool))
        att = jnp.where(causal, att, -jnp.inf)
        att = jax.nn.softmax(att, axis=-1)
        att = att * decay_weight_matrix(T)
        y = jnp.einsum('bhqk,bhkd->bhqd', att, v)
        y = y.transpose(0, 2, 1, 3).reshape(B, T, HEAD_QKV)
        return y @ W_proj

    def _L0_ffn_ref(hidden_states, W, b, lora_down, lora_up, down_aux, up_aux):
        import jax, jax.numpy as jnp
        import numpy as np
        ALPHA = 1.0
        lilora_weight = up_aux @ (lora_up @ (lora_down @ down_aux))
        base = jnp.einsum('bsi,oi->bso', hidden_states, W) + b
        delta = jnp.einsum('bsi,oi->bso', hidden_states, lilora_weight)
        return base + ALPHA * delta
    x = L0_attn_x
    mod = (_silu(L0_c) @ L0_wmod).reshape(L0_c.shape[0], 6, 1, -1)
    sa, ca, ga, sb, cb, gb = (mod[:, 0], mod[:, 1], mod[:, 2], mod[:, 3], mod[:, 4], mod[:, 5])
    ga = (2 * (ga >= 0) - 1) * jnp.maximum(jnp.abs(ga), 0.25)
    gb = (2 * (gb >= 0) - 1) * jnp.maximum(jnp.abs(gb), 0.25)
    h = _layernorm(x, axis=-1) * (1 + ca) + sa
    x = x + ga * _L0_attn_ref(h, L0_attn_W_attn, L0_attn_W_proj)
    h = _layernorm(x, axis=-1) * (1 + cb) + sb
    x = x + gb * _L0_ffn_ref(h, L0_ffn_W, L0_ffn_b, L0_ffn_lora_down, L0_ffn_lora_up, L0_ffn_down_aux, L0_ffn_up_aux)
    return x

_drawn_inputs = setup_inputs


def setup_inputs(seed=0):
    import zlib

    import numpy as np

    out = dict(_drawn_inputs(seed))
    spreads = {}
    factors = {'L0_attn_W_attn': 4.512,
     'L0_attn_W_proj': 4.462,
     'L0_ffn_b': 200.0,
     'L0_ffn_lora_down': 8.0,
     'L0_ffn_lora_up': 8.0,
     'L0_ffn_down_aux': 8.0,
     'L0_ffn_up_aux': 8.0,
     'L0_ffn_W': 8.0}
    for name, (base, spread) in spreads.items():
        noise = np.random.default_rng([zlib.crc32(name.encode()), seed]).standard_normal(out[name].shape)
        drawn = base * np.exp(spread * noise) if base else spread * noise
        out[name] = jnp.asarray(drawn.astype(out[name].dtype))
    for name, factor in factors.items():
        out[name] = (out[name] * factor).astype(out[name].dtype)
    return out
```

```python
import concourse.bass as bass
from concourse import mybir
from contextlib import ExitStack


def bass_adaln_block_kernel(nc, x, w_attn, w_proj, ffn_wT, ffn_b, lora_downT, lora_upT, down_aux, up_auxT,
                            cond_cols, w_mod, ident_in, causal_in, decay_rows, decay_cols, out):
    fp32 = mybir.dt.float32
    bf16 = mybir.dt.bfloat16
    ALU = mybir.AluOpType
    ACT = mybir.ActivationFunctionType
    AX_X = mybir.AxisListType.X

    P = 128
    T, C = x.shape
    CH = C // P
    NT = T // P
    NH, HD = 16, 16
    PARTS = 3
    PAIRS = [(0, 0), (0, 1), (0, 2), (1, 0), (1, 1), (2, 0)]
    SROWS = len(PAIRS) * HD
    G = 4
    GT = G * P
    NG = NT // G
    EPS = 1e-5
    BANK = 512
    CW = 2 * BANK
    RING = 3
    WIN = 5
    VR = 8
    SCORE_SCALE = -0.25

    def chunks(i):
        return -(-(i + 1) * P // CW)

    def chunk_keys(i, c):
        n = (i + 1) * P
        return max(0, n - CW * (c + 1)), n - CW * c

    def blocks(i):
        return min(WIN, i + 1)

    def jobs(i):
        nb = blocks(i)
        return [(0, min(3, nb))] + ([(3, nb)] if nb > 3 else [])

    NCMAX = chunks(NT - 1)
    first_multi = min(i for i in range(NT) if chunks(i) > 1)
    chunk_base = [0]
    for i in range(NT):
        chunk_base.append(chunk_base[-1] + NH * chunks(i))

    BY_ACT = [False, True, False]

    def count_units(i, q, s, kind):
        sel = [r for r in range(3) if BY_ACT[r] == kind]
        return q * len(sel) + sum(1 for r in sel if r < s)

    PER_TILE = {k: count_units(0, NH // 3, NH % 3, k) for k in (False, True)}
    unit_base = {k: [i * PER_TILE[k] for i in range(NT + 1)] for k in (False, True)}
    jobs_base = {k: [0] for k in (False, True)}
    alljobs_base = [0]
    for i in range(NT):
        for k in (False, True):
            jobs_base[k].append(jobs_base[k][-1] + len(jobs(i)) * PER_TILE[k])
        alljobs_base.append(alljobs_base[-1] + len(jobs(i)) * NH)

    class Unit:

        def __init__(self, i, q, s):
            self.i, self.q, self.s = i, q, s
            self.h = q * 3 + s
            self.nc = chunks(i)
            self.buf = (i * NH + s) % RING
            self.by_act = BY_ACT[s]
            self.jobs = jobs(i)

        def chunk(self, c):
            return self.h * self.nc + (chunk_base[self.i] + c)

        def units(self):
            return self.h + self.i * NH

        def kind_units(self):
            return count_units(self.i, self.q, self.s, self.by_act) + unit_base[self.by_act][self.i]

        def evacs(self, kind):
            return count_units(self.i, self.q, self.s, kind) * len(self.jobs) + jobs_base[kind][self.i]

        def all_jobs(self):
            return self.h * len(self.jobs) + alljobs_base[self.i]

        def back(self, lag):
            if isinstance(self.q, int):
                h = self.h - lag
                i = self.i
                if h < 0:
                    h, i = h + NH, i - 1
                return Unit(i, h // 3, h % 3) if i >= 0 else None
            s = self.s - lag
            return Unit(self.i, self.q + s // 3, s % 3)

    PEEL = 4

    def tile_units(eng, i, body):
        for h in range(PEEL):
            body(Unit(i, h // 3, h % 3), h)
        with eng.Fori(0, (NH - PEEL) // 3) as k:
            for r in range(3):
                s = PEEL + r
                body(Unit(i, k + s // 3, s % 3), None)

    TLAG, VLAG = 2, 3

    parts_d = nc.dram_tensor("parts_d", [PARTS, 2, C, T], bf16, kind="Internal").ap()
    v_d = nc.dram_tensor("v_d", [T, C], fp32, kind="Internal").ap()
    y_d = nc.dram_tensor("y_d", [T, C], fp32, kind="Internal").ap()
    x_tiles = x.rearrange("(t p) c -> p t c", p=P)
    v_tiles = v_d.rearrange("(t p) c -> p t c", p=P)
    y_tiles = y_d.rearrange("(t p) c -> p t c", p=P)
    out_tiles = out.rearrange("(t p) c -> p t c", p=P)

    ctx = ExitStack()
    with ctx:
        def sb(name, shape, dt, scope=ctx):
            return scope.enter_context(nc.sbuf_tensor(name, shape, dt))

        def sem(name):
            return ctx.enter_context(nc.semaphore(name))

        k_stack = sb("k_stack", [SROWS, NH, T], bf16)
        ident = sb("ident", [P, P], fp32)
        ident_b = sb("ident_b", [P, P], bf16)
        causal = sb("causal", [P, P], bf16)
        wp_g = sb("wp_g", [P, CH, C], fp32)
        wf_g = sb("wf_g", [P, CH, C], fp32)
        f_bias = sb("f_bias", [P, C], fp32)
        eps_t = sb("eps_t", [P, 1], fp32)

        w_loaded = sem("w_loaded")
        aux_loaded = sem("aux_loaded")
        x_loaded = [sem(f"x_loaded{g}") for g in range(NG)]
        v_step = sem("v_step")
        a_step = sem("a_step")
        pe_step = sem("pe_step")
        stats_ready = sem("stats_ready")
        std_ready = sem("std_ready")
        xn_ready = sem("xn_ready")
        xnT_ready = sem("xnT_ready")
        hT_by_act = sem("hT_by_act")
        hT_by_dve = sem("hT_by_dve")
        kq_ready = sem("kq_ready")
        v_ready = sem("v_ready")
        kq_out = sem("kq_out")
        v_out = sem("v_out")
        high_ready = sem("high_ready")
        rest1_ready = sem("rest1_ready")
        mid_ready = sem("mid_ready")
        low_ready = sem("low_ready")
        parts_stored = [sem(f"parts_stored{b}") for b in range(2)]
        v_stored = [sem(f"v_stored{b}") for b in range(2)]
        k_loaded = [sem(f"k_loaded{g}") for g in range(NG)]

        s1 = ExitStack()
        with s1:
            wmod_t = sb("wmod_t", [P, CH, 6 * C], fp32, s1)
            wa = sb("wa", [P, CH, 3 * C], fp32, s1)
            wa_f = wmod_t[:, :, 0:3 * C]
            ld_t = sb("ld_t", [100, 4], fp32, s1)
            lu_t = sb("lu_t", [4, 50], fp32, s1)
            da_t = sb("da_t", [100, C], fp32, s1)
            ua_t = sb("ua_t", [50, C], fp32, s1)
            b_row = sb("b_row", [1, C], fp32, s1)
            ones_t = sb("ones_t", [P, P], fp32, s1)
            cnd = sb("cnd", [P, CH], fp32, s1)
            sil = sb("sil", [P, CH], fp32, s1)
            tmp_c = sb("tmp_c", [P, CH], fp32, s1)
            sil_bc = sb("sil_bc", [P, CH, P], fp32, s1)
            sh_bc = sb("sh_bc", [P, 2, CH, P], fp32, s1)
            mod_c = sb("mod_c", [P, 4, CH], fp32, s1)
            gates = sb("gates", [P, 2, C], fp32, s1)
            kq_bias = sb("kq_bias", [P, 4], fp32, s1)
            v_bias = sb("v_bias", [P, C], fp32, s1)
            a2_t = sb("a2_t", [4, C], fp32, s1)
            a3_t = sb("a3_t", [50, C], fp32, s1)
            xs = sb("xs", [P, 2, G, C], fp32, s1)
            xn = sb("xn", [P, G, C], fp32, s1)
            gsign = xn[:, 0:2, :]
            st6 = sb("st6", [P, G, 6], fp32, s1)
            mv = sb("mv", [P, 2, G, 2], fp32, s1)
            sd = sb("sd", [P, 2, G], fp32, s1)
            rsd = sb("rsd", [P, 2, G], fp32, s1)
            hT = sb("hT", [P, CH, GT], fp32, s1)
            kq32 = sb("kq32", [P, 4, GT], fp32, s1)
            part = [sb(f"part{n}", [P, 4, GT], bf16, s1) for n in range(PARTS)]
            v_sb = sb("v_sb", [P, G, C], fp32, s1)
            pt_ps = s1.enter_context(nc.psum_tensor("pt_ps", [P, CH, GT], fp32))
            kq_ps = s1.enter_context(nc.psum_tensor("kq_ps", [P, 4, GT], fp32))
            v_ps = s1.enter_context(nc.psum_tensor("v_ps", [P, G, C], fp32))
            w_ps = kq_ps

            KQ_OFF = [C, C + P, 0, P]
            SHIFT_A, SCALE_A, SHIFT_B, SCALE_B = range(4)
            MOD_OF = [0, 1, 3, 4]

            wa_d = w_attn.rearrange("(h p) n -> p h n", p=P)
            PE_MOD, PE_BIAS, PE_A2, PE_A3, PE_LW, PE_FB = range(1, 7)
            V_EPS, V_SIL, V_SH, V_BIAS, V_A2, V_A3, V_WF, V_DONE = 2, 7, 13, 22, 27, 28, 30, 36

            block = s1.enter_context(nc.Block())

            @block.sync
            def _(sp):
                for dst, src in ((cnd[:], cond_cols), (wmod_t[:], w_mod.rearrange("(h p) n -> p h n", p=P)),
                                 (wa[:], wa_d), (ident[:], ident_in)):
                    sp.dma_start(dst, src).then_inc(w_loaded, 16)

                def load_x(g):
                    sp.dma_start(xs[:, g % 2], x_tiles[:, G * g:G * (g + 1), :]).then_inc(x_loaded[g], 16)

                load_x(0)
                load_x(1)
                for dst, src in ((wp_g[:], w_proj.rearrange("(h p) n -> p h n", p=P)),
                                 (wf_g[:], ffn_wT.rearrange("(h p) n -> p h n", p=P)),
                                 (ld_t[:], lora_downT), (lu_t[:], lora_upT), (da_t[:], down_aux),
                                 (ua_t[:], up_auxT), (b_row[:], ffn_b), (causal[:], causal_in)):
                    sp.dma_start(dst, src).then_inc(aux_loaded, 16)
                for g in range(NG):
                    for n, ready in ((0, high_ready), (1, mid_ready), (2, low_ready)):
                        sp.wait_ge(ready, g + 1)
                        for kq in range(2):
                            sp.dma_start(parts_d[n, kq].rearrange("(m p) t -> p m t", p=P)[:, :, GT * g:GT * (g + 1)],
                                         part[n][:, 2 * kq:2 * kq + 2, :]).then_inc(parts_stored[g % 2], 16)
                    sp.wait_ge(v_out, g + 1)
                    sp.dma_start(v_tiles[:, G * g:G * (g + 1), :], v_sb[:]).then_inc(v_stored[g % 2], 16)
                    if g + 2 < NG:
                        sp.wait_ge(xn_ready, g + 1)
                        load_x(g + 2)
                    sp.wait_ge(parts_stored[g % 2], 96 * (g // 2 + 1))
                    for j, (_, kp) in enumerate(PAIRS):
                        sp.dma_start(k_stack[HD * j:HD * (j + 1), :, GT * g:GT * (g + 1)],
                                     parts_d[kp, 0, :, GT * g:GT * (g + 1)].rearrange("(h d) t -> d h t", d=HD)
                                     ).then_inc(k_loaded[g], 16)


            @block.scalar
            def _(act):
                act.wait_ge(w_loaded, 64)
                nc.scalar.activation(tmp_c[:], cnd[:], ACT.Exp, scale=-1.0).then_inc(a_step, 1)
                act.wait_ge(v_step, V_EPS)
                for g in range(NG):
                    act.wait_ge(stats_ready, g + 1)
                    nc.scalar.activation(sd[:, g % 2, :], mv[:, g % 2, :, 1], ACT.Sqrt, bias=eps_t[:, 0:1]
                                         ).then_inc(std_ready, 1)
                    act.wait_ge(xnT_ready, g + 1)
                    if g >= 1:
                        act.wait_ge(v_ready, g)
                    nc.scalar.copy(hT[:, 0, :], pt_ps[:, 0, :]).then_inc(hT_by_act, 1)
                    if g == 0:
                        act.wait_ge(v_step, V_BIAS)
                    else:
                        act.wait_ge(low_ready, g)
                    for m in range(4):
                        act.wait_ge(kq_ready, 4 * g + m + 1)
                        nc.scalar.activation(kq32[:, m, :], kq_ps[:, m, :], ACT.Identity, bias=kq_bias[:, m:m + 1]
                                             ).then_inc(kq_out, 1)
                    act.wait_ge(kq_out, 4 * g + 4)
                    if g >= 1:
                        act.wait_ge(parts_stored[(g - 1) % 2], 96 * ((g - 1) // 2 + 1))
                    nc.scalar.copy(part[0][:], kq32[:]).then_inc(high_ready, 1)
                    act.wait_ge(rest1_ready, g + 1)
                    nc.scalar.copy(part[1][:], kq32[:]).then_inc(mid_ready, 1)

            @block.gpsimd
            def _(pool):
                for g in range(NG):
                    pool.wait_ge(mid_ready, g + 1)
                    nc.gpsimd.tensor_tensor(part[2][:], kq32[:], part[1][:], ALU.subtract).then_inc(low_ready, 1)

            steps = [0]

            @block.vector
            def _(dve):
                def step(ins):
                    steps[0] += 1
                    ins.then_inc(v_step, 1)
                    return steps[0]

                def serial(ins):
                    dve.wait_ge(v_step, step(ins))

                step(nc.vector.memset(ones_t[:], 1.0))
                serial(nc.vector.memset(eps_t[:], EPS))
                assert steps[0] == V_EPS
                dve.wait_ge(a_step, 1)
                serial(nc.vector.tensor_scalar_add(tmp_c[:], tmp_c[:], 1.0))
                serial(nc.vector.reciprocal(tmp_c[:], tmp_c[:]))
                serial(nc.vector.tensor_tensor(sil[:], cnd[:], tmp_c[:], ALU.mult))
                for cc in range(CH):
                    n = step(nc.vector.tensor_scalar(sil_bc[:, cc, :], ones_t[:], sil[:, cc:cc + 1], None, ALU.mult))
                assert n == V_SIL
                dve.wait_ge(pe_step, PE_MOD)
                serial(nc.vector.tensor_copy(mod_c[:], w_ps[:, 2, 0:8].rearrange("p (v h) -> p v h", h=CH)))
                g2 = gates[:].rearrange("p a c -> p (a c)")
                s2 = gsign.rearrange("p a c -> p (a c)")
                serial(nc.vector.tensor_copy(g2, w_ps[:, 0, :]))
                for a, v in ((0, SHIFT_A), (1, SHIFT_B)):
                    for cc in range(CH):
                        n = step(nc.vector.tensor_scalar(sh_bc[:, a, cc, :], ones_t[:], mod_c[:, v, cc:cc + 1], None, ALU.mult))
                assert n == V_SH
                for v in (SCALE_A, SCALE_B):
                    serial(nc.vector.tensor_scalar_add(mod_c[:, v, :], mod_c[:, v, :], 1.0))
                dve.wait_ge(pe_step, PE_BIAS)
                for cc in range(CH):
                    step(nc.vector.tensor_scalar(wa_f[:, cc, 0:C], wa[:, cc, 0:C], mod_c[:, SCALE_A, cc:cc + 1],
                                                 SCORE_SCALE, ALU.mult, ALU.mult))
                    step(nc.vector.tensor_scalar(wa_f[:, cc, C:3 * C], wa[:, cc, C:3 * C],
                                                 mod_c[:, SCALE_A, cc:cc + 1], None, ALU.mult))
                step(nc.vector.tensor_copy(kq_bias[:, 0:2], w_ps[:, 2, 0:2]))
                step(nc.vector.tensor_scalar(kq_bias[:, 2:4], w_ps[:, 2, 2:4], SCORE_SCALE, None, ALU.mult))
                serial(nc.vector.tensor_copy(v_bias[:], w_ps[:, 1, 0:C]))
                assert steps[0] == V_BIAS
                serial(nc.vector.tensor_scalar(s2, g2, 0.0, 2.0, ALU.is_ge, ALU.mult))
                serial(nc.vector.tensor_scalar_add(s2, s2, -1.0))
                serial(nc.vector.tensor_tensor(g2, g2, s2, ALU.mult))
                serial(nc.vector.scalar_tensor_tensor(g2, g2, 0.25, s2, ALU.max, ALU.mult))
                dve.wait_ge(pe_step, PE_A2)
                assert step(nc.vector.tensor_copy(a2_t[:], w_ps[0:4, 3, 0:C])) == V_A2
                dve.wait_ge(pe_step, PE_A3)
                assert step(nc.vector.tensor_copy(a3_t[:], w_ps[0:50, 3, 0:C])) == V_A3
                dve.wait_ge(pe_step, PE_LW)
                for cc in range(CH):
                    serial(nc.vector.tensor_tensor(wf_g[:, cc, :], wf_g[:, cc, :], w_ps[:, 3, C * cc:C * (cc + 1)], ALU.add))
                assert steps[0] == V_WF
                dve.wait_ge(aux_loaded, 128)
                dve.wait_ge(pe_step, PE_FB)
                for cc in range(CH):
                    step(nc.vector.tensor_tensor(wp_g[:, cc, :], wp_g[:, cc, :], gates[:, 0, :], ALU.mult))
                    step(nc.vector.scalar_tensor_tensor(wf_g[:, cc, :], wf_g[:, cc, :], mod_c[:, SCALE_B, cc:cc + 1],
                                                        gates[:, 1, :], ALU.mult, ALU.mult))
                step(nc.vector.tensor_tensor(f_bias[:], w_ps[:, 0, 0:C], gates[:, 1, :], ALU.mult))
                serial(nc.vector.tensor_copy(ident_b[:], ident[:]))
                assert steps[0] == V_DONE

                def stats(g):
                    dve.wait_ge(x_loaded[g], 16)
                    for t in range(G):
                        n = step(nc.vector.bn_stats(st6[:, t, :], xs[:, g % 2, t, :]))
                    dve.wait_ge(v_step, n)
                    for t in range(G):
                        last = nc.vector.bn_aggr(mv[:, g % 2, t, :], st6[:, t, :])
                        if t < G - 1:
                            step(last)
                    last.then_inc(stats_ready, 1)
                    dve.wait_ge(stats_ready, g + 1)

                stats(0)
                for g in range(NG):
                    if g + 1 < NG:
                        stats(g + 1)
                    dve.wait_ge(std_ready, g + 1)
                    serial(nc.vector.reciprocal(rsd[:, g % 2, :], sd[:, g % 2, :]))
                    if g >= 1:
                        dve.wait_ge(xnT_ready, g)
                    for t in range(G):
                        last = nc.vector.tensor_scalar(xn[:, t, :], xs[:, g % 2, t, :], mv[:, g % 2, t, 0:1],
                                                       rsd[:, g % 2, t:t + 1], ALU.subtract, ALU.mult)
                    last.then_inc(xn_ready, 1)
                    dve.wait_ge(xnT_ready, g + 1)
                    if g >= 1:
                        dve.wait_ge(v_ready, g)
                    nc.vector.tensor_copy(hT[:, 1, :], pt_ps[:, 1, :]).then_inc(hT_by_dve, 1)
                    dve.wait_ge(v_ready, g + 1)
                    if g >= 1:
                        dve.wait_ge(v_stored[(g - 1) % 2], 16 * ((g - 1) // 2 + 1))
                    nc.vector.tensor_tensor(v_sb[:], v_ps[:], v_bias[:].unsqueeze(1).to_broadcast([P, G, C]),
                                            ALU.add).then_inc(v_out, 1)
                    dve.wait_ge(high_ready, g + 1)
                    nc.vector.tensor_tensor(kq32[:], kq32[:], part[0][:], ALU.subtract).then_inc(rest1_ready, 1)

            @block.tensor
            def _(pe):
                pe.wait_ge(w_loaded, 64)
                pe.wait_ge(v_step, V_SIL)
                for a, v in ((0, 2), (1, 5)):
                    for cc in range(CH):
                        nc.tensor.matmul(w_ps[:, 0, C * a:C * (a + 1)], sil_bc[:, cc, :], wmod_t[:, cc, C * v:C * (v + 1)],
                                         start=(cc == 0), stop=(cc == CH - 1))
                for a, v in enumerate(MOD_OF):
                    for hf in range(CH):
                        for cc in range(CH):
                            last = nc.tensor.matmul(w_ps[:, 2, 2 * a + hf:2 * a + hf + 1],
                                                    wmod_t[:, cc, C * v + P * hf:C * v + P * (hf + 1)],
                                                    sil[:, cc:cc + 1], start=(cc == 0), stop=(cc == CH - 1))
                last.then_inc(pe_step, 1)
                pe.wait_ge(v_step, V_SH)
                for m in range(4):
                    for cc in range(CH):
                        nc.tensor.matmul(w_ps[:, 2, m:m + 1], wa[:, cc, KQ_OFF[m]:KQ_OFF[m] + P],
                                         mod_c[:, SHIFT_A, cc:cc + 1], start=(cc == 0), stop=(cc == CH - 1))
                for cc in range(CH):
                    last = nc.tensor.matmul(w_ps[:, 1, 0:C], sh_bc[:, 0, cc, :], wa[:, cc, 2 * C:3 * C],
                                            start=(cc == 0), stop=(cc == CH - 1))
                last.then_inc(pe_step, 1)
                pe.wait_ge(aux_loaded, 128)
                nc.tensor.matmul(w_ps[0:4, 3, 0:C], ld_t[:], da_t[:], start=True, stop=True).then_inc(pe_step, 1)
                pe.wait_ge(v_step, V_A2)
                nc.tensor.matmul(w_ps[0:50, 3, 0:C], lu_t[:], a2_t[:], start=True, stop=True).then_inc(pe_step, 1)
                pe.wait_ge(v_step, V_A3)
                for cc in range(CH):
                    last = nc.tensor.matmul(w_ps[:, 3, C * cc:C * (cc + 1)], a3_t[:, P * cc:P * (cc + 1)], ua_t[:],
                                            start=True, stop=True)
                last.then_inc(pe_step, 1)
                pe.wait_ge(v_step, V_WF)
                for cc in range(CH):
                    nc.tensor.matmul(w_ps[:, 0, 0:C], sh_bc[:, 1, cc, :], wf_g[:, cc, :], start=(cc == 0), stop=False)
                nc.tensor.matmul(w_ps[:, 0, 0:C], ones_t[0:1, :], b_row[:], start=False, stop=True).then_inc(pe_step, 1)
                pe.wait_ge(v_step, V_DONE)
                for g in range(NG):
                    pe.wait_ge(xn_ready, g + 1)
                    if g >= 1:
                        pe.wait_ge(hT_by_act, g)
                        pe.wait_ge(hT_by_dve, g)
                    for t in range(G):
                        for cc in range(CH):
                            last = nc.tensor.transpose(pt_ps[:, cc, P * t:P * (t + 1)], xn[:, t, P * cc:P * (cc + 1)], ident[:])
                    last.then_inc(xnT_ready, 1)
                    pe.wait_ge(hT_by_act, g + 1)
                    pe.wait_ge(hT_by_dve, g + 1)
                    for m in range(4):
                        if g >= 1:
                            pe.wait_ge(kq_out, 4 * (g - 1) + m + 1)
                        for cc in range(CH):
                            last = nc.tensor.matmul(kq_ps[:, m, :], wa_f[:, cc, KQ_OFF[m]:KQ_OFF[m] + P], hT[:, cc, :],
                                                    start=(cc == 0), stop=(cc == CH - 1))
                        last.then_inc(kq_ready, 1)
                    if g >= 1:
                        pe.wait_ge(v_out, g)
                    for t in range(G):
                        for cc in range(CH):
                            last = nc.tensor.matmul(v_ps[:, t, :], hT[:, cc, P * t:P * (t + 1)], wa_f[:, cc, 2 * C:3 * C],
                                                    start=(cc == 0), stop=(cc == CH - 1))
                    last.then_inc(v_ready, 1)

        q_loaded = [sem(f"q_loaded{b}") for b in range(2)]
        vals_loaded = [sem(f"vals_loaded{b}") for b in range(2)]
        decay_loaded = sem("decay_loaded")
        chunk_ready = sem("chunk_ready")
        max_ready = sem("max_ready")
        exp_done = sem("exp_done")
        decayed = sem("decayed")
        job_ready = sem("job_ready")
        job_out = {False: sem("job_out_dve"), True: sem("job_out_act")}
        unit_done = sem("unit_done")
        spread_ready = sem("spread_ready")
        weight_ready = sem("weight_ready")
        y_out = sem("y_out")
        y_stored = [sem(f"y_stored{b}") for b in range(2)]
        t_step = sem("t_step")

        s2 = ExitStack()
        with s2:
            q_stack = sb("q_stack", [SROWS, 2, NH, 2 * P], bf16, s2)
            probs = sb("probs", [P, RING, CW], fp32, s2)
            probsT = sb("probsT", [P, RING, WIN, P], fp32, s2)
            vals = sb("vals", [P, VR, C], fp32, s2)
            dec_r = sb("dec_r", [P, WIN * P], fp32, s2)
            dec_c = sb("dec_c", [P, WIN, P], fp32, s2)
            y_sb = sb("y_sb", [P, 2, C], fp32, s2)
            negmax = sb("negmax", [P, 2, NH, NCMAX], fp32, s2)
            sums = sb("sums", [P, 2, NH, NCMAX], fp32, s2)
            negtop = sb("negtop", [P, NH], fp32, s2)
            spread = sb("spread", [P, NH, NCMAX], fp32, s2)
            weight = sb("weight", [P, NH, NCMAX], fp32, s2)
            scaled = sb("scaled", [P, NH, NCMAX], fp32, s2)
            total = sb("total", [P, NH], fp32, s2)
            factor = sb("factor", [P, NH], fp32, s2)
            s_ps = s2.enter_context(nc.psum_tensor("s_ps", [P, RING, CW], fp32))
            t_ps = s2.enter_context(nc.psum_tensor("t_ps", [P, BANK], fp32))
            y_ps = s2.enter_context(nc.psum_tensor("y_ps", [P, BANK], fp32))
            block = s2.enter_context(nc.Block())

            @block.sync
            def _(sp):
                sp.dma_start(dec_r[:], decay_rows).then_inc(decay_loaded, 16)
                sp.dma_start(dec_c[:], decay_cols).then_inc(decay_loaded, 16)

                def store_y(i):
                    sp.wait_ge(y_out, i + 1)
                    sp.dma_start(y_tiles[:, i, :], y_sb[:, i % 2, :]).then_inc(y_stored[i % 2], 16)

                for m in range(NT // 2):
                    if m >= 2:
                        sp.wait_ge(chunk_ready, chunk_base[2 * m - 2])
                    for j, (qp, _) in enumerate(PAIRS):
                        sp.dma_start(q_stack[HD * j:HD * (j + 1), m % 2, :, :],
                                     parts_d[qp, 1, :, 2 * P * m:2 * P * (m + 1)].rearrange("(h d) t -> d h t", d=HD)
                                     ).then_inc(q_loaded[m % 2], 16)
                    if m >= VR // 2:
                        sp.wait_ge(unit_done, NH * (2 * m - VR + WIN + 1))
                    sp.dma_start(vals[:, (2 * m) % VR:(2 * m) % VR + 2, :], v_tiles[:, 2 * m:2 * m + 2, :]
                                 ).then_inc(vals_loaded[m % 2], 16)
                    for i in (2 * m - 4, 2 * m - 3):
                        if i >= 0:
                            store_y(i)
                for i in range(NT - 4, NT):
                    store_y(i)
                for b in range(2):
                    sp.wait_ge(y_stored[b], 16 * (NT // 2))

            def score_unit_chunk(pe, u, c):
                k0, k1 = chunk_keys(u.i, c)
                b = (chunk_base[u.i] + c + u.s * u.nc) % RING
                if c == 0 or True:
                    need = u.chunk(c) - (RING - 1)
                    if not isinstance(need, int) or need > 0:
                        pe.wait_ge(exp_done, need)
                q = q_stack[:, (u.i // 2) % 2, u.h, P * (u.i % 2):P * (u.i % 2 + 1)]
                for o in range(0, k1 - k0, BANK):
                    n = min(BANK, k1 - k0 - o)
                    diag = c == 0 and k0 + o + n == k1
                    last = nc.tensor.matmul(s_ps[:, b, o:o + n], q, k_stack[:, u.h, k0 + o:k0 + o + n],
                                            start=True, stop=not diag)
                    if diag:
                        last = nc.tensor.matmul(s_ps[:, b, o + n - P:o + n], ident_b[:], causal[:], start=False, stop=True)
                last.then_inc(chunk_ready, 1)

            def transpose_job(pe, u, j):
                if j == 0:
                    if u.by_act:
                        pe.wait_ge(decayed, u.kind_units() + 1)
                    else:
                        pe.wait_ge(exp_done, u.chunk(0) + 1)
                prev = u if j > 0 else u.back(1)
                if prev is not None:
                    pe.wait_ge(job_out[prev.by_act], prev.evacs(prev.by_act) + (j if j > 0 else len(prev.jobs)))
                w0 = min(CW, (u.i + 1) * P)
                b0, b1 = u.jobs[j]
                for b in range(b0, b1):
                    lo = w0 - P * (blocks(u.i) - b)
                    last = nc.tensor.transpose(t_ps[:, P * (b - b0):P * (b - b0 + 1)], probs[:, u.buf, lo:lo + P], ident[:])
                last.then_inc(job_ready, 1)

            def values_product(pe, u):
                pe.wait_ge(job_out[u.by_act], u.evacs(u.by_act) + len(u.jobs))
                nb = blocks(u.i)
                for b in range(nb):
                    kt = u.i + 1 - nb + b
                    last = nc.tensor.matmul(y_ps[:, bass.ds(u.h * HD, HD)], probsT[:, u.buf, b, :],
                                            vals[:, kt % VR, bass.ds(u.h * HD, HD)], start=(b == 0), stop=(b == nb - 1))
                last.then_inc(unit_done, 1)

            @block.tensor
            def _(pe):
                def body(u, peeled):
                    t, v = u.back(TLAG), u.back(VLAG)
                    if peeled == 0:
                        if u.i % 2 == 0:
                            pe.wait_ge(q_loaded[(u.i // 2) % 2], 96 * (u.i // 4 + 1))
                        if u.i % G == 0:
                            pe.wait_ge(k_loaded[u.i // G], 96)
                    if peeled == VLAG:
                        if u.i % 2 == 0:
                            pe.wait_ge(vals_loaded[(u.i // 2) % 2], 16 * (u.i // 4 + 1))
                        if u.i >= 1:
                            pe.wait_ge(y_out, u.i)
                    score_unit_chunk(pe, u, 0)
                    if t is not None:
                        transpose_job(pe, t, 0)
                    if v is not None:
                        values_product(pe, v)
                    if u.nc > 1:
                        score_unit_chunk(pe, u, 1)
                    if t is not None and len(t.jobs) > 1:
                        transpose_job(pe, t, 1)
                    for c in range(2, u.nc):
                        score_unit_chunk(pe, u, c)

                for i in range(NT):
                    tile_units(pe, i, body)
                end = Unit(NT - 1, NH // 3, NH % 3)
                for lag in range(VLAG):
                    t, v = end.back(TLAG - lag) if lag < TLAG else None, end.back(VLAG - lag)
                    if t is not None:
                        transpose_job(pe, t, 0)
                    values_product(pe, v)
                    if t is not None:
                        transpose_job(pe, t, 1)

            def evacuate(eng, u, j, by_act):
                if u is None or u.by_act != by_act or j >= len(u.jobs):
                    return
                if j == 0:
                    need = u.units() - (RING - 1)
                    if not isinstance(need, int) or need > 0:
                        eng.wait_ge(unit_done, need)
                eng.wait_ge(job_ready, u.all_jobs() + j + 1)
                b0, b1 = u.jobs[j]
                dst = probsT[:, u.buf, b0:b1, :]
                src = t_ps[:, 0:P * (b1 - b0)].rearrange("p (b q) -> p b q", q=P)
                if by_act:
                    ins = nc.scalar.copy(dst, src)
                else:
                    d0 = WIN - blocks(u.i) + b0
                    ins = nc.vector.tensor_tensor(dst, src, dec_c[:, d0:d0 + b1 - b0, :], ALU.mult)
                ins.then_inc(job_out[by_act], 1)

            @block.scalar
            def _(act):
                def exponential(u, c):
                    k0, k1 = chunk_keys(u.i, c)
                    b = (chunk_base[u.i] + c + u.s * u.nc) % RING
                    act.wait_ge(max_ready, u.chunk(c) + 1)
                    par = u.i % 2
                    src = s_ps[:, b, 0:k1 - k0]
                    dst = src
                    if c == 0:
                        old = u.back(RING)
                        if old is not None:
                            act.wait_ge(job_ready, old.all_jobs() + len(old.jobs))
                        dst = probs[:, u.buf, 0:k1 - k0]
                    nc.scalar.activation(dst, src, ACT.Exp, bias=negmax[:, par, u.h, c:c + 1], scale=-1.0,
                                         accum_out=sums[:, par, u.h, c:c + 1]).then_inc(exp_done, 1)

                def weights(i):
                    act.wait_ge(spread_ready, i + 1 - first_multi)
                    n = chunks(i)
                    nc.scalar.activation(weight[:, :, 0:n], spread[:, :, 0:n], ACT.Exp).then_inc(weight_ready, 1)

                def body(u, peeled):
                    t = u.back(TLAG)
                    exponential(u, 0)
                    evacuate(act, t, 0, True)
                    if u.nc > 1:
                        exponential(u, 1)
                    evacuate(act, t, 1, True)
                    for c in range(2, u.nc):
                        exponential(u, c)
                    if peeled == 0 and u.i > 0 and chunks(u.i - 1) > 1:
                        weights(u.i - 1)

                for i in range(NT):
                    tile_units(act, i, body)
                end = Unit(NT - 1, NH // 3, NH % 3)
                for lag in range(TLAG, 0, -1):
                    for j in range(2):
                        evacuate(act, end.back(lag), j, True)
                weights(NT - 1)

            @block.gpsimd
            def _(pool):
                pool.wait_ge(decay_loaded, 32)

                def body(u, peeled):
                    if not u.by_act:
                        return
                    w0 = min(CW, (u.i + 1) * P)
                    n = P * blocks(u.i)
                    pool.wait_ge(exp_done, u.chunk(0) + 1)
                    p = probs[:, u.buf, w0 - n:w0]
                    nc.gpsimd.tensor_tensor(p, p, dec_r[:, WIN * P - n:], ALU.mult).then_inc(decayed, 1)

                for i in range(NT):
                    tile_units(pool, i, body)

            tsteps = [0]

            @block.vector
            def _(dve):
                dve.wait_ge(decay_loaded, 32)

                def serial(ins):
                    tsteps[0] += 1
                    ins.then_inc(t_step, 1)
                    dve.wait_ge(t_step, tsteps[0])

                def maximum(u, c):
                    k0, k1 = chunk_keys(u.i, c)
                    b = (chunk_base[u.i] + c + u.s * u.nc) % RING
                    dve.wait_ge(chunk_ready, u.chunk(c) + 1)
                    nc.vector.tensor_reduce(out=negmax[:, u.i % 2, u.h, c:c + 1], in_=s_ps[:, b, 0:k1 - k0],
                                            axis=AX_X, op=ALU.min).then_inc(max_ready, 1)

                def spreads(i):
                    n = chunks(i)
                    dve.wait_ge(max_ready, chunk_base[i + 1])
                    if i > first_multi:
                        dve.wait_ge(weight_ready, i - first_multi)
                    serial(nc.vector.tensor_reduce(out=negtop[:], in_=negmax[:, i % 2, :, 0:n], axis=AX_X, op=ALU.min))
                    nc.vector.tensor_tensor(spread[:, :, 0:n], negtop[:].unsqueeze(2).to_broadcast([P, NH, n]),
                                            negmax[:, i % 2, :, 0:n], ALU.subtract).then_inc(spread_ready, 1)

                def factors(i):
                    n = chunks(i)
                    dve.wait_ge(exp_done, chunk_base[i + 1])
                    if n == 1:
                        serial(nc.vector.reciprocal(factor[:], sums[:, i % 2, :, 0]))
                        return
                    dve.wait_ge(weight_ready, i + 1 - first_multi)
                    serial(nc.vector.tensor_tensor(scaled[:, :, 0:n], weight[:, :, 0:n], sums[:, i % 2, :, 0:n], ALU.mult))
                    serial(nc.vector.reduce_sum(total[:], scaled[:, :, 0:n], axis=AX_X))
                    serial(nc.vector.reciprocal(total[:], total[:]))
                    serial(nc.vector.tensor_tensor(factor[:], total[:], weight[:, :, 0], ALU.mult))

                def finish(i):
                    dve.wait_ge(unit_done, NH * (i + 1))
                    if i >= 2:
                        dve.wait_ge(y_stored[i % 2], 16 * (i // 2))
                    nc.vector.tensor_tensor(y_sb[:, i % 2, :].rearrange("p (h d) -> p h d", d=HD),
                                            y_ps[:, 0:C].rearrange("p (h d) -> p h d", d=HD),
                                            factor[:].unsqueeze(2).to_broadcast([P, NH, HD]), ALU.mult).then_inc(y_out, 1)

                def body(u, peeled):
                    t = u.back(TLAG)
                    maximum(u, 0)
                    evacuate(dve, t, 0, False)
                    if u.nc > 1:
                        maximum(u, 1)
                    evacuate(dve, t, 1, False)
                    for c in range(2, u.nc):
                        maximum(u, c)
                    if u.i > 0:
                        if peeled == 0 and chunks(u.i - 1) > 1:
                            spreads(u.i - 1)
                        if peeled == 1:
                            factors(u.i - 1)
                        if peeled == VLAG - 1:
                            finish(u.i - 1)

                for i in range(NT):
                    tile_units(dve, i, body)
                end = Unit(NT - 1, NH // 3, NH % 3)
                for lag in range(TLAG, 0, -1):
                    for j in range(2):
                        evacuate(dve, end.back(lag), j, False)
                spreads(NT - 1)
                factors(NT - 1)
                finish(NT - 1)

        B3 = 2
        NB = NT // B3
        xy_loaded = [sem(f"xy_loaded{b}") for b in range(2)]
        yT_ready = sem("yT_ready")
        yT_out = sem("yT_out")
        att_ready = sem("att_ready")
        x2_done = sem("x2_done")
        var_ready = sem("var_ready")
        dev_ready = sem("dev_ready")
        n_ready = sem("n_ready")
        nT_ready = sem("nT_ready")
        nT_out = sem("nT_out")
        ff_ready = sem("ff_ready")
        biased = sem("biased")
        o_ready = sem("o_ready")
        o_stored = [sem(f"o_stored{b}") for b in range(2)]
        r_step = sem("r_step")

        s3 = ExitStack()
        with s3:
            x_sb = sb("x_sb", [P, 2, B3, C], fp32, s3)
            yy = sb("yy", [P, 2, B3, C], fp32, s3)
            yT = sb("yT", [P, 2, B3, CH, P], fp32, s3)
            x2 = sb("x2", [P, 2, B3, C], fp32, s3)
            x2b = sb("x2b", [P, 2, B3, C], fp32, s3)
            nrm = sb("nrm", [P, 2, B3, C], fp32, s3)
            nT = sb("nT", [P, 2, B3, CH, P], fp32, s3)
            o_sb = sb("o_sb", [P, 2, B3, C], fp32, s3)
            q6 = sb("q6", [P, B3, 6], fp32, s3)
            mv3 = sb("mv3", [P, 2, B3, 2], fp32, s3)
            sd3 = sb("sd3", [P, 2, B3], fp32, s3)
            rs3 = sb("rs3", [P, 2, B3], fp32, s3)
            yT_ps = s3.enter_context(nc.psum_tensor("yT_ps", [P, 2, B3, CH, P], fp32))
            at_ps = s3.enter_context(nc.psum_tensor("at_ps", [P, 2, B3, C], fp32))
            nT_ps = s3.enter_context(nc.psum_tensor("nT_ps", [P, 2, B3, CH, P], fp32))
            ff_ps = s3.enter_context(nc.psum_tensor("ff_ps", [P, 2, B3, C], fp32))
            block = s3.enter_context(nc.Block())

            @block.sync
            def _(sp):
                def load(m):
                    sp.dma_start(yy[:, m % 2], y_tiles[:, B3 * m:B3 * (m + 1), :]).then_inc(xy_loaded[m % 2], 16)
                    sp.dma_start(x_sb[:, m % 2], x_tiles[:, B3 * m:B3 * (m + 1), :]).then_inc(xy_loaded[m % 2], 16)

                load(0)
                load(1)
                for m in range(NB):
                    if m + 2 < NB:
                        sp.wait_ge(x2_done, m + 1)
                        load(m + 2)
                    sp.wait_ge(o_ready, m + 1)
                    sp.dma_start(out_tiles[:, B3 * m:B3 * (m + 1), :], o_sb[:, m % 2]).then_inc(o_stored[m % 2], 16)
                for b in range(2):
                    sp.wait_ge(o_stored[b], 16 * (NB // 2))

            @block.tensor
            def _(pe):
                def half_a(m):
                    b = m % 2
                    pe.wait_ge(xy_loaded[b], 32 * (m // 2 + 1))
                    if m >= 2:
                        pe.wait_ge(yT_out, m - 1)
                    for t in range(B3):
                        for cc in range(CH):
                            last = nc.tensor.transpose(yT_ps[:, b, t, cc, :], yy[:, b, t, P * cc:P * (cc + 1)], ident[:])
                    last.then_inc(yT_ready, 1)
                    pe.wait_ge(yT_out, m + 1)
                    if m >= 2:
                        pe.wait_ge(x2_done, m - 1)
                    for t in range(B3):
                        for cc in range(CH):
                            last = nc.tensor.matmul(at_ps[:, b, t, :], yT[:, b, t, cc, :], wp_g[:, cc, :],
                                                    start=(cc == 0), stop=(cc == CH - 1))
                    last.then_inc(att_ready, 1)

                def half_b(m):
                    b = m % 2
                    pe.wait_ge(n_ready, m + 1)
                    if m >= 2:
                        pe.wait_ge(nT_out, m - 1)
                    for t in range(B3):
                        for cc in range(CH):
                            last = nc.tensor.transpose(nT_ps[:, b, t, cc, :], nrm[:, b, t, P * cc:P * (cc + 1)], ident[:])
                    last.then_inc(nT_ready, 1)
                    pe.wait_ge(nT_out, m + 1)
                    if m >= 2:
                        pe.wait_ge(o_ready, m - 1)
                    for t in range(B3):
                        for cc in range(CH):
                            last = nc.tensor.matmul(ff_ps[:, b, t, :], nT[:, b, t, cc, :], wf_g[:, cc, :],
                                                    start=(cc == 0), stop=(cc == CH - 1))
                    last.then_inc(ff_ready, 1)

                half_a(0)
                for m in range(NB):
                    if m + 1 < NB:
                        half_a(m + 1)
                    half_b(m)

            @block.scalar
            def _(act):
                def half_a(m):
                    b = m % 2
                    act.wait_ge(yT_ready, m + 1)
                    if m >= 2:
                        act.wait_ge(att_ready, m - 1)
                    nc.scalar.copy(yT[:, b], yT_ps[:, b]).then_inc(yT_out, 1)
                    act.wait_ge(var_ready, m + 1)
                    if m >= 2:
                        act.wait_ge(n_ready, m - 1)
                    nc.scalar.activation(sd3[:, b, :], mv3[:, b, :, 1], ACT.Sqrt, bias=eps_t[:, 0:1]).then_inc(dev_ready, 1)

                def half_b(m):
                    b = m % 2
                    act.wait_ge(nT_ready, m + 1)
                    if m >= 2:
                        act.wait_ge(ff_ready, m - 1)
                    nc.scalar.copy(nT[:, b], nT_ps[:, b]).then_inc(nT_out, 1)

                half_a(0)
                for m in range(NB):
                    if m + 1 < NB:
                        half_a(m + 1)
                    half_b(m)

            @block.gpsimd
            def _(pool):
                for m in range(NB):
                    b = m % 2
                    pool.wait_ge(x2_done, m + 1)
                    if m >= 2:
                        pool.wait_ge(o_ready, m - 1)
                    nc.gpsimd.tensor_tensor(x2b[:, b], x2[:, b], f_bias[:].unsqueeze(1).to_broadcast([P, B3, C]),
                                            ALU.add).then_inc(biased, 1)

            rsteps = [0]

            @block.vector
            def _(dve):
                def serial(ins):
                    rsteps[0] += 1
                    ins.then_inc(r_step, 1)
                    dve.wait_ge(r_step, rsteps[0])

                def half_a(m):
                    b = m % 2
                    dve.wait_ge(att_ready, m + 1)
                    dve.wait_ge(xy_loaded[b], 32 * (m // 2 + 1))
                    if m >= 2:
                        dve.wait_ge(biased, m - 1)
                    nc.vector.tensor_tensor(x2[:, b], x_sb[:, b], at_ps[:, b], ALU.add).then_inc(x2_done, 1)
                    dve.wait_ge(x2_done, m + 1)
                    for t in range(B3):
                        last = nc.vector.bn_stats(q6[:, t, :], x2[:, b, t, :])
                    serial(last)
                    for t in range(B3):
                        last = nc.vector.bn_aggr(mv3[:, b, t, :], q6[:, t, :])
                    last.then_inc(var_ready, 1)

                def half_a2(m):
                    b = m % 2
                    dve.wait_ge(dev_ready, m + 1)
                    serial(nc.vector.reciprocal(rs3[:, b, :], sd3[:, b, :]))
                    if m >= 2:
                        dve.wait_ge(nT_ready, m - 1)
                    dve.wait_ge(var_ready, m + 1)
                    for t in range(B3):
                        last = nc.vector.tensor_scalar(nrm[:, b, t, :], x2[:, b, t, :], mv3[:, b, t, 0:1], rs3[:, b, t:t + 1],
                                                       ALU.subtract, ALU.mult)
                    last.then_inc(n_ready, 1)

                def half_b(m):
                    b = m % 2
                    dve.wait_ge(ff_ready, m + 1)
                    dve.wait_ge(biased, m + 1)
                    if m >= 2:
                        dve.wait_ge(o_stored[b], 16 * (m // 2))
                    nc.vector.tensor_tensor(o_sb[:, b], ff_ps[:, b], x2b[:, b], ALU.add).then_inc(o_ready, 1)

                half_a(0)
                half_a2(0)
                for m in range(NB):
                    if m + 1 < NB:
                        half_a(m + 1)
                        half_a2(m + 1)
                    half_b(m)


def kernel(**inputs):
    import numpy as _np
    import concourse.bacc as _bacc
    from concourse import mybir as _mybir
    from concourse.bass_utils import run_bass_kernel_spmd as _run

    def a(name):
        return _np.asarray(inputs[name])

    P, WIN, LENGTH, ECHOIC = 128, 5, 512, 16
    ramp = _np.linspace(0.0, 1.0, LENGTH - ECHOIC + 1).astype(_np.float32)
    decay = 1.0 - _np.power(ramp, _np.float32(1.0 / _np.e))
    decay = _np.concatenate([_np.ones(ECHOIC - 1), decay]).astype(_np.float32)
    dist = _np.arange(P)[:, None] + P * (WIN - 1) - _np.arange(P * WIN)[None, :]
    rows = _np.where((dist >= 0) & (dist < LENGTH), decay[_np.clip(dist, 0, LENGTH - 1)], 0).astype(_np.float32)
    cols = rows.reshape(P, WIN, P).transpose(2, 1, 0)
    bf16 = _mybir.dt.np(_mybir.dt.bfloat16)
    causal = _np.where(_np.arange(P)[None, :] > _np.arange(P)[:, None], 1e30, 0.0).astype(bf16)

    ins = {
        "x": a("L0_attn_x")[0],
        "w_attn": a("L0_attn_W_attn"), "w_proj": a("L0_attn_W_proj"),
        "ffn_wT": a("L0_ffn_W").T, "ffn_b": a("L0_ffn_b")[None, :],
        "lora_downT": a("L0_ffn_lora_down").T, "lora_upT": a("L0_ffn_lora_up").T,
        "down_aux": a("L0_ffn_down_aux"), "up_auxT": a("L0_ffn_up_aux").T,
        "cond_cols": a("L0_c").reshape(2, P).T, "w_mod": a("L0_wmod"),
        "ident_in": _np.eye(P, dtype=_np.float32), "causal_in": causal, "decay_rows": rows, "decay_cols": cols,
    }
    nc = _bacc.Bacc("TRN2", target_bir_lowering=False, num_devices=1)
    arrays, args = {}, []
    for name, v in ins.items():
        v = _np.ascontiguousarray(v)
        arrays[f"{name}_dram"] = v
        args.append(nc.dram_tensor(f"{name}_dram", v.shape, _mybir.dt.from_np(v.dtype), kind="ExternalInput").ap())
    out = nc.dram_tensor("out_dram", ins["x"].shape, _mybir.dt.float32, kind="ExternalOutput").ap()
    bass_adaln_block_kernel(nc, *args, out)
    r = _run(nc, [arrays], core_ids=[0])
    return r.results[0]["out_dram"][None]
```

```python
import concourse.bass as bass
from concourse import mybir
from contextlib import ExitStack


def bass_adaln_block_kernel(nc, x, w_attn, w_proj, ffn_wT, ffn_b, lora_downT, lora_upT, down_aux, up_auxT,
                            cond_cols, w_mod, ident_in, causal_in, decay_rows, decay_cols, out):
    fp32 = mybir.dt.float32
    bf16 = mybir.dt.bfloat16
    ALU = mybir.AluOpType
    ACT = mybir.ActivationFunctionType
    AX_X = mybir.AxisListType.X

    P = 128
    T, C = x.shape
    CH = C // P
    NT = T // P
    NH, HD = 16, 16
    PARTS = 3
    PAIRS = [(0, 0), (0, 1), (0, 2), (1, 0), (1, 1), (2, 0)]
    SROWS = len(PAIRS) * HD
    G = 4
    GT = G * P
    NG = NT // G
    EPS = 1e-5
    BANK = 512
    CW = 2 * BANK
    RING = 3
    WIN = 5
    VR = 8
    SCORE_SCALE = -0.25

    def chunks(i):
        return -(-(i + 1) * P // CW)

    def chunk_keys(i, c):
        n = (i + 1) * P
        return max(0, n - CW * (c + 1)), n - CW * c

    def blocks(i):
        return min(WIN, i + 1)

    def jobs(i):
        nb = blocks(i)
        return [(0, min(3, nb))] + ([(3, nb)] if nb > 3 else [])

    NCMAX = chunks(NT - 1)
    first_multi = min(i for i in range(NT) if chunks(i) > 1)
    chunk_base = [0]
    for i in range(NT):
        chunk_base.append(chunk_base[-1] + NH * chunks(i))

    BY_ACT = [False, True, False]

    def count_units(i, q, s, kind):
        sel = [r for r in range(3) if BY_ACT[r] == kind]
        return q * len(sel) + sum(1 for r in sel if r < s)

    PER_TILE = {k: count_units(0, NH // 3, NH % 3, k) for k in (False, True)}
    unit_base = {k: [i * PER_TILE[k] for i in range(NT + 1)] for k in (False, True)}
    jobs_base = {k: [0] for k in (False, True)}
    alljobs_base = [0]
    for i in range(NT):
        for k in (False, True):
            jobs_base[k].append(jobs_base[k][-1] + len(jobs(i)) * PER_TILE[k])
        alljobs_base.append(alljobs_base[-1] + len(jobs(i)) * NH)

    class Unit:

        def __init__(self, i, q, s):
            self.i, self.q, self.s = i, q, s
            self.h = q * 3 + s
            self.nc = chunks(i)
            self.buf = (i * NH + s) % RING
            self.by_act = BY_ACT[s]
            self.jobs = jobs(i)

        def chunk(self, c):
            return self.h * self.nc + (chunk_base[self.i] + c)

        def units(self):
            return self.h + self.i * NH

        def kind_units(self):
            return count_units(self.i, self.q, self.s, self.by_act) + unit_base[self.by_act][self.i]

        def evacs(self, kind):
            return count_units(self.i, self.q, self.s, kind) * len(self.jobs) + jobs_base[kind][self.i]

        def slot(self):
            return (self.s - 1) % 3

        def groups_before_reuse(self):
            if isinstance(self.h, int) and self.h < 2:
                return self.i * GROUPS
            return self.q + (self.i * GROUPS + 1 + (self.s - 1) // 3)

        def groups_issued(self):
            if isinstance(self.h, int) and self.h < 2:
                return self.i * GROUPS + self.h
            return self.q + (self.i * GROUPS + (self.s + 2) // 3)

        def all_jobs(self):
            return self.h * len(self.jobs) + alljobs_base[self.i]

        def back(self, lag):
            if isinstance(self.q, int):
                h = self.h - lag
                i = self.i
                if h < 0:
                    h, i = h + NH, i - 1
                return Unit(i, h // 3, h % 3) if i >= 0 else None
            s = self.s - lag
            return Unit(self.i, self.q + s // 3, s % 3)

    PEEL = 4

    def tile_units(eng, i, body):
        for h in range(PEEL):
            body(Unit(i, h // 3, h % 3), h)
        with eng.Fori(0, (NH - PEEL) // 3) as k:
            for r in range(3):
                s = PEEL + r
                body(Unit(i, k + s // 3, s % 3), None)

    TLAG = 2
    GROUPS = 1 + (NH - 1) // 3

    def paired(eng, n, body):
        for g in (0, 1):
            body(g, g, 0, g, n - 1 - g)
        with eng.Fori(1, n // 2 - 1) as k:
            for b in range(2):
                body(k * 2 + b, b, k, 2, 2)
        for g in (n - 2, n - 1):
            body(g, g % 2, g // 2, 2, n - 1 - g)

    parts_d = nc.dram_tensor("parts_d", [PARTS, 2, C, T], bf16, kind="Internal").ap()
    v_d = nc.dram_tensor("v_d", [T, C], fp32, kind="Internal").ap()
    y_d = nc.dram_tensor("y_d", [T, C], fp32, kind="Internal").ap()
    x_tiles = x.rearrange("(t p) c -> p t c", p=P)
    v_tiles = v_d.rearrange("(t p) c -> p t c", p=P)
    y_tiles = y_d.rearrange("(t p) c -> p t c", p=P)
    out_tiles = out.rearrange("(t p) c -> p t c", p=P)

    ctx = ExitStack()
    with ctx:
        def sb(name, shape, dt, scope=ctx):
            return scope.enter_context(nc.sbuf_tensor(name, shape, dt))

        def sem(name):
            return ctx.enter_context(nc.semaphore(name))

        k_stack = sb("k_stack", [SROWS, NH, T], bf16)
        ident = sb("ident", [P, P], fp32)
        ident_b = sb("ident_b", [P, P], bf16)
        causal = sb("causal", [P, P], bf16)
        wp_g = sb("wp_g", [P, CH, C], fp32)
        wf_g = sb("wf_g", [P, CH, C], fp32)
        f_bias = sb("f_bias", [P, C], fp32)
        eps_t = sb("eps_t", [P, 1], fp32)

        w_loaded = sem("w_loaded")
        aux_loaded = sem("aux_loaded")
        x_loaded = [sem(f"x_loaded{b}") for b in range(2)]
        v_step = sem("v_step")
        a_step = sem("a_step")
        pe_step = sem("pe_step")
        stat6_done = sem("stat6_done")
        stats_ready = sem("stats_ready")
        std_ready = sem("std_ready")
        rstd_done = sem("rstd_done")
        xn_ready = sem("xn_ready")
        xnT_ready = sem("xnT_ready")
        hT_by_act = sem("hT_by_act")
        hT_by_dve = sem("hT_by_dve")
        kq_ready = sem("kq_ready")
        v_ready = sem("v_ready")
        kq_out = sem("kq_out")
        v_out = sem("v_out")
        high_ready = sem("high_ready")
        rest1_ready = sem("rest1_ready")
        mid_ready = sem("mid_ready")
        low_ready = sem("low_ready")
        parts_stored = [sem(f"parts_stored{b}") for b in range(2)]
        v_stored = [sem(f"v_stored{b}") for b in range(2)]
        k_loaded = sem("k_loaded")

        s1 = ExitStack()
        with s1:
            w0 = sb("w0", [P, 9 * CH * C], fp32, s1)
            wmod_t = w0[:, 0:6 * CH * C].rearrange("p (h n) -> p h n", h=CH)
            wa = w0[:, 6 * CH * C:].rearrange("p (h n) -> p h n", h=CH)
            wa_f = w0[:, 0:3 * CH * C].rearrange("p (h n) -> p h n", h=CH)
            hT_odd = w0[:, 3 * CH * C:3 * CH * C + CH * GT].rearrange("p (h t) -> p h t", h=CH)
            v_sb = w0[:, 6 * CH * C:6 * CH * C + G * C].rearrange("p (t c) -> p t c", t=G)
            ld_t = sb("ld_t", [100, 4], fp32, s1)
            lu_t = sb("lu_t", [4, 50], fp32, s1)
            da_t = sb("da_t", [100, C], fp32, s1)
            ua_t = sb("ua_t", [50, C], fp32, s1)
            b_row = sb("b_row", [1, C], fp32, s1)
            ones_t = sb("ones_t", [P, P], fp32, s1)
            cnd = sb("cnd", [P, CH], fp32, s1)
            sil = sb("sil", [P, CH], fp32, s1)
            tmp_c = sb("tmp_c", [P, CH], fp32, s1)
            kq32 = sb("kq32", [P, 2, 4, GT], fp32, s1)
            sil_bc = kq32[:, 0, 0, 0:CH * P].rearrange("p (h n) -> p h n", h=CH)
            sh_bc = kq32[:, 0, 1, 0:2 * CH * P].rearrange("p (a h n) -> p a h n", a=2, h=CH)
            mod_c = sb("mod_c", [P, 4, CH], fp32, s1)
            gates = sb("gates", [P, 2, C], fp32, s1)
            kq_bias = sb("kq_bias", [P, 4], fp32, s1)
            v_bias = sb("v_bias", [P, C], fp32, s1)
            a2_t = sb("a2_t", [4, C], fp32, s1)
            a3_t = sb("a3_t", [50, C], fp32, s1)
            xs = sb("xs", [P, 2, G, C], fp32, s1)
            xn = sb("xn", [P, G, C], fp32, s1)
            gsign = xn[:, 0:2, :]
            st6 = sb("st6", [P, 2, G, 6], fp32, s1)
            mv = sb("mv", [P, 2, G, 2], fp32, s1)
            sd = sb("sd", [P, 2, G], fp32, s1)
            rsd = sb("rsd", [P, 2, G], fp32, s1)
            hT = [sb("hT", [P, CH, GT], fp32, s1)[:], hT_odd]
            part = [sb(f"part{n}", [P, 4, GT], bf16, s1) for n in range(PARTS)]
            pt_ps = s1.enter_context(nc.psum_tensor("pt_ps", [P, CH, GT], fp32))
            kq_ps = s1.enter_context(nc.psum_tensor("kq_ps", [P, 4, GT], fp32))
            v_ps = s1.enter_context(nc.psum_tensor("v_ps", [P, G, C], fp32))
            w_ps = kq_ps

            KQ_OFF = [C, C + P, 0, P]
            SHIFT_A, SCALE_A, SHIFT_B, SCALE_B = range(4)
            MOD_OF = [0, 1, 3, 4]

            wa_d = w_attn.rearrange("(h p) n -> p h n", p=P)
            PE_MOD, PE_BIAS, PE_A2, PE_A3, PE_LW, PE_FB = range(1, 7)
            V_EPS, V_SIL, V_SH, V_BIAS, V_A2, V_A3, V_WF, V_DONE = 2, 7, 13, 22, 27, 28, 30, 36

            block = s1.enter_context(nc.Block())

            @block.sync
            def _(sp):
                for dst, src in ((cnd[:], cond_cols), (wmod_t, w_mod.rearrange("(h p) n -> p h n", p=P)),
                                 (wa, wa_d), (ident[:], ident_in)):
                    sp.dma_start(dst, src).then_inc(w_loaded, 16)

                def load_x(g, b):
                    sp.dma_start(xs[:, b], x_tiles[:, bass.ds(g * G, G), :]).then_inc(x_loaded[b], 16)

                load_x(0, 0)
                load_x(1, 1)
                for dst, src in ((wp_g[:], w_proj.rearrange("(h p) n -> p h n", p=P)),
                                 (wf_g[:], ffn_wT.rearrange("(h p) n -> p h n", p=P)),
                                 (ld_t[:], lora_downT), (lu_t[:], lora_upT), (da_t[:], down_aux),
                                 (ua_t[:], up_auxT), (b_row[:], ffn_b), (causal[:], causal_in)):
                    sp.dma_start(dst, src).then_inc(aux_loaded, 16)

                def body(g, b, k, first, last):
                    tok = bass.ds(g * GT, GT)
                    if last >= 2:
                        sp.wait_ge(xn_ready, g + 1)
                        load_x(g + 2, b)
                    for n, ready in ((0, high_ready), (None, v_out), (1, mid_ready), (2, low_ready)):
                        sp.wait_ge(ready, g + 1)
                        if n is None:
                            sp.dma_start(v_tiles[:, bass.ds(g * G, G), :], v_sb).then_inc(v_stored[b], 16)
                            continue
                        for kq in range(2):
                            sp.dma_start(parts_d[n, kq].rearrange("(m p) t -> p m t", p=P)[:, :, tok],
                                         part[n][:, 2 * kq:2 * kq + 2, :]).then_inc(parts_stored[b], 16)
                    sp.wait_ge(parts_stored[b], (k + 1) * 96)
                    for j, (_, kp) in enumerate(PAIRS):
                        sp.dma_start(k_stack[HD * j:HD * (j + 1), :, tok],
                                     parts_d[kp, 0, :, tok].rearrange("(h d) t -> d h t", d=HD)).then_inc(k_loaded, 16)

                for g in range(NG):
                    body(g, g % 2, g // 2, min(g, 2), min(NG - 1 - g, 2))
                sp.wait_ge(k_loaded, 16 * len(PAIRS) * NG)
                for b in range(2):
                    sp.wait_ge(v_stored[b], 16 * (NG // 2))

            @block.scalar
            def _(act):
                act.wait_ge(w_loaded, 64)
                nc.scalar.activation(tmp_c[:], cnd[:], ACT.Exp, scale=-1.0).then_inc(a_step, 1)
                act.wait_ge(v_step, V_EPS)

                def std(g, b):
                    act.wait_ge(stats_ready, g + 1)
                    nc.scalar.activation(sd[:, b, :], mv[:, b, :, 1], ACT.Sqrt, bias=eps_t[:, 0:1]).then_inc(std_ready, 1)

                def half_hT(g, b):
                    act.wait_ge(xnT_ready, g + 1)
                    nc.scalar.copy(hT[b][:, 0, :], pt_ps[:, 0, :]).then_inc(hT_by_act, 1)

                std(0, 0)
                act.wait_ge(v_step, V_BIAS)
                half_hT(0, 0)
                std(1, 1)

                def body(g, b, k, first, last):
                    if first >= 2:
                        act.wait_ge(low_ready, g - 1)
                    elif first == 0:
                        act.wait_ge(v_step, V_DONE)
                    for m in range(4):
                        act.wait_ge(kq_ready, g * 4 + (m + 1))
                        nc.scalar.activation(kq32[:, b, m, :], kq_ps[:, m, :], ACT.Identity, bias=kq_bias[:, m:m + 1]
                                             ).then_inc(kq_out, 1)
                    if last >= 1:
                        if first >= 1:
                            act.wait_ge(v_ready, g)
                        half_hT(g + 1, 1 - b)
                    if first >= 1:
                        act.wait_ge(parts_stored[1 - b], (k + b) * 96)
                    act.wait_ge(kq_out, g * 4 + 4)
                    nc.scalar.copy(part[0][:], kq32[:, b]).then_inc(high_ready, 1)
                    if last >= 2:
                        std(g + 2, b)
                    act.wait_ge(rest1_ready, g + 1)
                    nc.scalar.copy(part[1][:], kq32[:, b]).then_inc(mid_ready, 1)

                paired(act, NG, body)

            @block.gpsimd
            def _(pool):
                def body(g, b, k, first, last):
                    pool.wait_ge(mid_ready, g + 1)
                    nc.gpsimd.tensor_tensor(part[2][:], kq32[:, b], part[1][:], ALU.subtract).then_inc(low_ready, 1)

                paired(pool, NG, body)

            steps = [0]

            @block.vector
            def _(dve):
                def step(ins):
                    steps[0] += 1
                    ins.then_inc(v_step, 1)
                    return steps[0]

                def serial(ins):
                    dve.wait_ge(v_step, step(ins))

                step(nc.vector.memset(ones_t[:], 1.0))
                serial(nc.vector.memset(eps_t[:], EPS))
                assert steps[0] == V_EPS
                dve.wait_ge(a_step, 1)
                serial(nc.vector.tensor_scalar_add(tmp_c[:], tmp_c[:], 1.0))
                serial(nc.vector.reciprocal(tmp_c[:], tmp_c[:]))
                serial(nc.vector.tensor_tensor(sil[:], cnd[:], tmp_c[:], ALU.mult))
                for cc in range(CH):
                    n = step(nc.vector.tensor_scalar(sil_bc[:, cc, :], ones_t[:], sil[:, cc:cc + 1], None, ALU.mult))
                assert n == V_SIL
                dve.wait_ge(pe_step, PE_MOD)
                serial(nc.vector.tensor_copy(mod_c[:], w_ps[:, 2, 0:8].rearrange("p (v h) -> p v h", h=CH)))
                g2 = gates[:].rearrange("p a c -> p (a c)")
                s2 = gsign.rearrange("p a c -> p (a c)")
                serial(nc.vector.tensor_copy(g2, w_ps[:, 0, :]))
                for a, v in ((0, SHIFT_A), (1, SHIFT_B)):
                    for cc in range(CH):
                        n = step(nc.vector.tensor_scalar(sh_bc[:, a, cc, :], ones_t[:], mod_c[:, v, cc:cc + 1], None, ALU.mult))
                assert n == V_SH
                for v in (SCALE_A, SCALE_B):
                    serial(nc.vector.tensor_scalar_add(mod_c[:, v, :], mod_c[:, v, :], 1.0))
                dve.wait_ge(pe_step, PE_BIAS)
                for cc in range(CH):
                    step(nc.vector.tensor_scalar(wa_f[:, cc, 0:C], wa[:, cc, 0:C], mod_c[:, SCALE_A, cc:cc + 1],
                                                 SCORE_SCALE, ALU.mult, ALU.mult))
                    step(nc.vector.tensor_scalar(wa_f[:, cc, C:3 * C], wa[:, cc, C:3 * C],
                                                 mod_c[:, SCALE_A, cc:cc + 1], None, ALU.mult))
                step(nc.vector.tensor_copy(kq_bias[:, 0:2], w_ps[:, 2, 0:2]))
                step(nc.vector.tensor_scalar(kq_bias[:, 2:4], w_ps[:, 2, 2:4], SCORE_SCALE, None, ALU.mult))
                serial(nc.vector.tensor_copy(v_bias[:], w_ps[:, 1, 0:C]))
                assert steps[0] == V_BIAS
                serial(nc.vector.tensor_scalar(s2, g2, 0.0, 2.0, ALU.is_ge, ALU.mult))
                serial(nc.vector.tensor_scalar_add(s2, s2, -1.0))
                serial(nc.vector.tensor_tensor(g2, g2, s2, ALU.mult))
                serial(nc.vector.scalar_tensor_tensor(g2, g2, 0.25, s2, ALU.max, ALU.mult))
                dve.wait_ge(pe_step, PE_A2)
                assert step(nc.vector.tensor_copy(a2_t[:], w_ps[0:4, 3, 0:C])) == V_A2
                dve.wait_ge(pe_step, PE_A3)
                assert step(nc.vector.tensor_copy(a3_t[:], w_ps[0:50, 3, 0:C])) == V_A3
                dve.wait_ge(pe_step, PE_LW)
                for cc in range(CH):
                    serial(nc.vector.tensor_tensor(wf_g[:, cc, :], wf_g[:, cc, :], w_ps[:, 3, C * cc:C * (cc + 1)], ALU.add))
                assert steps[0] == V_WF
                dve.wait_ge(aux_loaded, 128)
                dve.wait_ge(pe_step, PE_FB)
                for cc in range(CH):
                    step(nc.vector.tensor_tensor(wp_g[:, cc, :], wp_g[:, cc, :], gates[:, 0, :], ALU.mult))
                    step(nc.vector.scalar_tensor_tensor(wf_g[:, cc, :], wf_g[:, cc, :], mod_c[:, SCALE_B, cc:cc + 1],
                                                        gates[:, 1, :], ALU.mult, ALU.mult))
                step(nc.vector.tensor_tensor(f_bias[:], w_ps[:, 0, 0:C], gates[:, 1, :], ALU.mult))
                serial(nc.vector.tensor_copy(ident_b[:], ident[:]))
                assert steps[0] == V_DONE

                def stats(g, b, k):
                    dve.wait_ge(x_loaded[b], (k + 1) * 16)
                    for t in range(G):
                        last = nc.vector.bn_stats(st6[:, b, t, :], xs[:, b, t, :])
                    last.then_inc(stat6_done, 1)

                def means(g, b):
                    for t in range(G):
                        last = nc.vector.bn_aggr(mv[:, b, t, :], st6[:, b, t, :])
                    last.then_inc(stats_ready, 1)

                def normalise(g, b):
                    dve.wait_ge(std_ready, g + 1)
                    nc.vector.reciprocal(rsd[:, b, :], sd[:, b, :]).then_inc(rstd_done, 1)
                    dve.wait_ge(rstd_done, g + 1)
                    for t in range(G):
                        last = nc.vector.tensor_scalar(xn[:, t, :], xs[:, b, t, :], mv[:, b, t, 0:1],
                                                       rsd[:, b, t:t + 1], ALU.subtract, ALU.mult)
                    last.then_inc(xn_ready, 1)

                def half_hT(g, b):
                    dve.wait_ge(xnT_ready, g + 1)
                    nc.vector.tensor_copy(hT[b][:, 1, :], pt_ps[:, 1, :]).then_inc(hT_by_dve, 1)

                stats(0, 0, 0)
                dve.wait_ge(stat6_done, 1)
                means(0, 0)
                stats(1, 1, 0)
                dve.wait_ge(stat6_done, 2)
                means(1, 1)
                dve.wait_ge(stats_ready, 1)
                normalise(0, 0)
                half_hT(0, 0)

                def body(g, b, k, first, last):
                    if last >= 1:
                        dve.wait_ge(xnT_ready, g + 1)
                        dve.wait_ge(stats_ready, g + 2)
                        normalise(g + 1, 1 - b)
                    if last >= 2:
                        stats(g + 2, b, k + 1)
                    if last >= 1:
                        if first >= 1:
                            dve.wait_ge(v_ready, g)
                        if last >= 2:
                            dve.wait_ge(stat6_done, g + 3)
                        half_hT(g + 1, 1 - b)
                    if last >= 2:
                        means(g + 2, b)
                    dve.wait_ge(high_ready, g + 1)
                    nc.vector.tensor_tensor(kq32[:, b], kq32[:, b], part[0][:], ALU.subtract).then_inc(rest1_ready, 1)
                    dve.wait_ge(v_ready, g + 1)
                    if first >= 1:
                        dve.wait_ge(v_stored[1 - b], (k + b) * 16)
                    nc.vector.tensor_tensor(v_sb, v_ps[:], v_bias[:].unsqueeze(1).to_broadcast([P, G, C]),
                                            ALU.add).then_inc(v_out, 1)

                paired(dve, NG, body)

            @block.tensor
            def _(pe):
                pe.wait_ge(w_loaded, 64)
                pe.wait_ge(v_step, V_SIL)
                for a, v in ((0, 2), (1, 5)):
                    for cc in range(CH):
                        nc.tensor.matmul(w_ps[:, 0, C * a:C * (a + 1)], sil_bc[:, cc, :], wmod_t[:, cc, C * v:C * (v + 1)],
                                         start=(cc == 0), stop=(cc == CH - 1))
                for a, v in enumerate(MOD_OF):
                    for hf in range(CH):
                        for cc in range(CH):
                            last = nc.tensor.matmul(w_ps[:, 2, 2 * a + hf:2 * a + hf + 1],
                                                    wmod_t[:, cc, C * v + P * hf:C * v + P * (hf + 1)],
                                                    sil[:, cc:cc + 1], start=(cc == 0), stop=(cc == CH - 1))
                last.then_inc(pe_step, 1)
                pe.wait_ge(v_step, V_SH)
                for m in range(4):
                    for cc in range(CH):
                        nc.tensor.matmul(w_ps[:, 2, m:m + 1], wa[:, cc, KQ_OFF[m]:KQ_OFF[m] + P],
                                         mod_c[:, SHIFT_A, cc:cc + 1], start=(cc == 0), stop=(cc == CH - 1))
                for cc in range(CH):
                    last = nc.tensor.matmul(w_ps[:, 1, 0:C], sh_bc[:, 0, cc, :], wa[:, cc, 2 * C:3 * C],
                                            start=(cc == 0), stop=(cc == CH - 1))
                last.then_inc(pe_step, 1)
                pe.wait_ge(aux_loaded, 128)
                nc.tensor.matmul(w_ps[0:4, 3, 0:C], ld_t[:], da_t[:], start=True, stop=True).then_inc(pe_step, 1)
                pe.wait_ge(v_step, V_A2)
                nc.tensor.matmul(w_ps[0:50, 3, 0:C], lu_t[:], a2_t[:], start=True, stop=True).then_inc(pe_step, 1)
                pe.wait_ge(v_step, V_A3)
                for cc in range(CH):
                    last = nc.tensor.matmul(w_ps[:, 3, C * cc:C * (cc + 1)], a3_t[:, P * cc:P * (cc + 1)], ua_t[:],
                                            start=True, stop=True)
                last.then_inc(pe_step, 1)
                pe.wait_ge(v_step, V_WF)
                for cc in range(CH):
                    nc.tensor.matmul(w_ps[:, 0, 0:C], sh_bc[:, 1, cc, :], wf_g[:, cc, :], start=(cc == 0), stop=False)
                nc.tensor.matmul(w_ps[:, 0, 0:C], ones_t[0:1, :], b_row[:], start=False, stop=True).then_inc(pe_step, 1)
                pe.wait_ge(v_step, V_DONE)

                def transposes(g):
                    pe.wait_ge(xn_ready, g + 1)
                    for t in range(G):
                        for cc in range(CH):
                            last = nc.tensor.transpose(pt_ps[:, cc, P * t:P * (t + 1)], xn[:, t, P * cc:P * (cc + 1)], ident[:])
                    last.then_inc(xnT_ready, 1)

                transposes(0)

                def body(g, b, k, first, last):
                    pe.wait_ge(hT_by_act, g + 1)
                    pe.wait_ge(hT_by_dve, g + 1)
                    for m in range(4):
                        if first >= 1:
                            pe.wait_ge(kq_out, g * 4 + (m - 3))
                        for cc in range(CH):
                            mm = nc.tensor.matmul(kq_ps[:, m, :], wa_f[:, cc, KQ_OFF[m]:KQ_OFF[m] + P], hT[b][:, cc, :],
                                                  start=(cc == 0), stop=(cc == CH - 1))
                        mm.then_inc(kq_ready, 1)
                    if last >= 1:
                        transposes(g + 1)
                    if first >= 1:
                        pe.wait_ge(v_out, g)
                    for t in range(G):
                        for cc in range(CH):
                            mm = nc.tensor.matmul(v_ps[:, t, :], hT[b][:, cc, P * t:P * (t + 1)], wa_f[:, cc, 2 * C:3 * C],
                                                  start=(cc == 0), stop=(cc == CH - 1))
                    mm.then_inc(v_ready, 1)

                paired(pe, NG, body)

        q_loaded = [sem(f"q_loaded{b}") for b in range(2)]
        vals_loaded = [sem(f"vals_loaded{b}") for b in range(2)]
        decay_loaded = sem("decay_loaded")
        chunk_ready = sem("chunk_ready")
        max_ready = sem("max_ready")
        exp_done = sem("exp_done")
        decayed = sem("decayed")
        job_ready = sem("job_ready")
        job_out = {False: sem("job_out_dve"), True: sem("job_out_act")}
        staged = sem("staged")
        group_done = sem("group_done")
        group_out = sem("group_out")
        back_ready = sem("back_ready")
        spread_ready = sem("spread_ready")
        weight_ready = sem("weight_ready")
        y_out = sem("y_out")
        y_stored = [sem(f"y_stored{b}") for b in range(2)]
        t_step = sem("t_step")
        zeroed = sem("zeroed")

        s2 = ExitStack()
        with s2:
            q_stack = sb("q_stack", [SROWS, 2, NH, 2 * P], bf16, s2)
            probs = sb("probs", [P, RING, CW], fp32, s2)
            probsT = sb("probsT", [P, RING, WIN, P], fp32, s2)
            vals = sb("vals", [P, VR, C], fp32, s2)
            dec_r = sb("dec_r", [P, WIN * P], fp32, s2)
            dec_c = sb("dec_c", [P, WIN, P], fp32, s2)
            TC = 32
            vstage0 = sb("vstage0", [P, WIN, 1, TC], fp32, s2)
            vstage = sb("vstage", [P, WIN, 3, TC], fp32, s2)
            yT_sb = sb("yT_sb", [3 * TC, GROUPS, P], fp32, s2)
            y_sb = sb("y_sb", [P, 2, C], fp32, s2)
            negmax = sb("negmax", [P, 2, NH, NCMAX], fp32, s2)
            sums = sb("sums", [P, 2, NH, NCMAX], fp32, s2)
            negtop = sb("negtop", [P, NH], fp32, s2)
            spread = sb("spread", [P, NH, NCMAX], fp32, s2)
            weight = sb("weight", [P, NH, NCMAX], fp32, s2)
            scaled = sb("scaled", [P, NH, NCMAX], fp32, s2)
            total = sb("total", [P, NH], fp32, s2)
            factor = sb("factor", [P, NH], fp32, s2)
            s_ps = s2.enter_context(nc.psum_tensor("s_ps", [P, RING, CW], fp32))
            t_ps = s2.enter_context(nc.psum_tensor("t_ps", [P, 2, BANK], fp32))
            g_ps = t_ps[:, 1, :]
            block = s2.enter_context(nc.Block())

            @block.sync
            def _(sp):
                sp.dma_start(dec_r[:], decay_rows).then_inc(decay_loaded, 16)
                sp.dma_start(dec_c[:], decay_cols).then_inc(decay_loaded, 16)

                def store_y(i):
                    sp.wait_ge(y_out, i + 1)
                    sp.dma_start(y_tiles[:, i, :], y_sb[:, i % 2, :]).then_inc(y_stored[i % 2], 16)

                for m in range(NT // 2):
                    if m >= 2:
                        sp.wait_ge(chunk_ready, chunk_base[2 * m - 2])
                    for j, (qp, _) in enumerate(PAIRS):
                        sp.dma_start(q_stack[HD * j:HD * (j + 1), m % 2, :, :],
                                     parts_d[qp, 1, :, 2 * P * m:2 * P * (m + 1)].rearrange("(h d) t -> d h t", d=HD)
                                     ).then_inc(q_loaded[m % 2], 16)
                    if m >= VR // 2:
                        sp.wait_ge(staged, GROUPS * (2 * m - VR + WIN + 1))
                    sp.dma_start(vals[:, (2 * m) % VR:(2 * m) % VR + 2, :], v_tiles[:, 2 * m:2 * m + 2, :]
                                 ).then_inc(vals_loaded[m % 2], 16)
                    for i in (2 * m - 4, 2 * m - 3):
                        if i >= 0:
                            store_y(i)
                for i in range(NT - 4, NT):
                    store_y(i)
                for b in range(2):
                    sp.wait_ge(y_stored[b], 16 * (NT // 2))

            def score_chunk(pe, u, c):
                k0, k1 = chunk_keys(u.i, c)
                b = (chunk_base[u.i] + c + u.s * u.nc) % RING
                need = u.chunk(c) - (RING - 1)
                if not isinstance(need, int) or need > 0:
                    pe.wait_ge(exp_done, need)
                q = q_stack[:, (u.i // 2) % 2, u.h, P * (u.i % 2):P * (u.i % 2 + 1)]
                for o in range(0, k1 - k0, BANK):
                    n = min(BANK, k1 - k0 - o)
                    diag = c == 0 and k0 + o + n == k1
                    last = nc.tensor.matmul(s_ps[:, b, o:o + n], q, k_stack[:, u.h, k0 + o:k0 + o + n],
                                            start=True, stop=not diag)
                    if diag:
                        last = nc.tensor.matmul(s_ps[:, b, o + n - P:o + n], ident_b[:], causal[:], start=False, stop=True)
                last.then_inc(chunk_ready, 1)

            def transpose_job(pe, u, j):
                if j == 0:
                    if u.by_act:
                        pe.wait_ge(decayed, u.kind_units() + 1)
                    else:
                        pe.wait_ge(exp_done, u.chunk(0) + 1)
                prev = u.back(1)
                if prev is not None and j < len(prev.jobs):
                    pe.wait_ge(job_out[prev.by_act], prev.evacs(prev.by_act) + j + 1)
                if j == 0 and isinstance(u.h, int) and u.h == 1 and u.i > 0:
                    pe.wait_ge(y_out, u.i)
                if j == 1:
                    pe.wait_ge(group_out, u.groups_issued())
                w0 = min(CW, (u.i + 1) * P)
                b0, b1 = u.jobs[j]
                for b in range(b0, b1):
                    lo = w0 - P * (blocks(u.i) - b)
                    last = nc.tensor.transpose(t_ps[:, j, P * (b - b0):P * (b - b0 + 1)], probs[:, u.buf, lo:lo + P], ident[:])
                last.then_inc(job_ready, 1)

            def group_heads(u):
                return [u] if isinstance(u.h, int) and u.h == 0 else [u.back(2), u.back(1), u]

            def values_group(pe, u):
                n = u.q + u.i * GROUPS
                after = Unit(u.i, u.q, u.s + 1)
                for kind in (False, True):
                    pe.wait_ge(job_out[kind], after.evacs(kind))
                pe.wait_ge(staged, n + 1)
                if not (isinstance(n, int) and n == 0):
                    pe.wait_ge(group_out, n)
                heads = group_heads(u)
                vs = vstage0 if len(heads) == 1 else vstage
                nb = blocks(u.i)
                for b in range(nb):
                    for j, v in enumerate(heads):
                        last = nc.tensor.matmul(g_ps[TC * j:TC * (j + 1), 0:P], vs[:, b, j, :],
                                                probsT[:, v.slot(), b, :], start=(b == 0), stop=(b == nb - 1))
                last.then_inc(group_done, 1)

            def turn_back(pe, i):
                last_t = Unit(i + 1, 0, 0) if i + 1 < NT else Unit(i, (NH - 1) // 3, (NH - 1) % 3)
                k = last_t.by_act
                pe.wait_ge(job_out[k], last_t.evacs(k) + 1)
                pe.wait_ge(group_out, GROUPS * (i + 1))
                for g in range(GROUPS):
                    w = TC if g == 0 else 3 * TC
                    o = 0 if g == 0 else TC + 3 * TC * (g - 1)
                    last = nc.tensor.transpose(t_ps[:, 0, o:o + w], yT_sb[0:w, g, :], ident[0:w, 0:w])
                last.then_inc(back_ready, 1)

            @block.tensor
            def _(pe):
                def body(u, peeled):
                    t = u.back(TLAG)
                    if peeled == 0 and u.i % 2 == 0:
                        pe.wait_ge(q_loaded[(u.i // 2) % 2], 96 * (u.i // 4 + 1))
                    score_chunk(pe, u, 0)
                    if peeled is None and u.s == 0:
                        values_group(pe, u.back(3))
                    if peeled == 2 and u.i > 0:
                        values_group(pe, Unit(u.i - 1, (NH - 1) // 3, 0))
                    if peeled == 3:
                        if u.i > 0:
                            turn_back(pe, u.i - 1)
                        values_group(pe, Unit(u.i, 0, 0))
                    if t is not None:
                        transpose_job(pe, t, 0)
                    if u.nc > 1:
                        score_chunk(pe, u, 1)
                    if t is not None and len(t.jobs) > 1:
                        transpose_job(pe, t, 1)
                    for c in range(2, u.nc):
                        score_chunk(pe, u, c)

                for i in range(NT):
                    tile_units(pe, i, body)
                for h in (NH - 2, NH - 1):
                    for j in range(2):
                        transpose_job(pe, Unit(NT - 1, h // 3, h % 3), j)
                values_group(pe, Unit(NT - 1, (NH - 1) // 3, 0))
                turn_back(pe, NT - 1)

            def evacuate(eng, u, j, by_act):
                if u is None or u.by_act != by_act or j >= len(u.jobs):
                    return
                if j == 0:
                    need = u.groups_before_reuse()
                    if not isinstance(need, int) or need > 0:
                        eng.wait_ge(group_done, need)
                eng.wait_ge(job_ready, u.all_jobs() + j + 1)
                b0, b1 = u.jobs[j]
                dst = probsT[:, u.slot(), b0:b1, :]
                src = t_ps[:, j, 0:P * (b1 - b0)].rearrange("p (b q) -> p b q", q=P)
                if by_act:
                    ins = nc.scalar.copy(dst, src)
                else:
                    d0 = WIN - blocks(u.i) + b0
                    ins = nc.vector.tensor_tensor(dst, src, dec_c[:, d0:d0 + b1 - b0, :], ALU.mult)
                ins.then_inc(job_out[by_act], 1)

            @block.scalar
            def _(act):
                def exponential(u, c):
                    k0, k1 = chunk_keys(u.i, c)
                    b = (chunk_base[u.i] + c + u.s * u.nc) % RING
                    act.wait_ge(max_ready, u.chunk(c) + 1)
                    par = u.i % 2
                    src = s_ps[:, b, 0:k1 - k0]
                    dst = src
                    if c == 0:
                        old = u.back(RING)
                        if old is not None:
                            act.wait_ge(job_ready, old.all_jobs() + len(old.jobs))
                        dst = probs[:, u.buf, 0:k1 - k0]
                    nc.scalar.activation(dst, src, ACT.Exp, bias=negmax[:, par, u.h, c:c + 1], scale=-1.0,
                                         accum_out=sums[:, par, u.h, c:c + 1]).then_inc(exp_done, 1)

                def weights(i):
                    act.wait_ge(spread_ready, i + 1 - first_multi)
                    n = chunks(i)
                    nc.scalar.activation(weight[:, :, 0:n], spread[:, :, 0:n], ACT.Exp).then_inc(weight_ready, 1)

                def body(u, peeled):
                    t = u.back(TLAG)
                    exponential(u, 0)
                    evacuate(act, t, 0, True)
                    if u.nc > 1:
                        exponential(u, 1)
                    evacuate(act, t, 1, True)
                    for c in range(2, u.nc):
                        exponential(u, c)
                    if peeled == 0 and u.i > 0 and chunks(u.i - 1) > 1:
                        weights(u.i - 1)

                for i in range(NT):
                    tile_units(act, i, body)
                end = Unit(NT - 1, NH // 3, NH % 3)
                for lag in range(TLAG, 0, -1):
                    for j in range(2):
                        evacuate(act, end.back(lag), j, True)
                weights(NT - 1)

            @block.gpsimd
            def _(pool):
                nc.gpsimd.memset(vstage0[:], 0.0).then_inc(zeroed, 1)
                nc.gpsimd.memset(vstage[:], 0.0).then_inc(zeroed, 1)
                pool.wait_ge(zeroed, 2)
                pool.wait_ge(decay_loaded, 32)

                def decay(u):
                    w0 = min(CW, (u.i + 1) * P)
                    n = P * blocks(u.i)
                    pool.wait_ge(exp_done, u.chunk(0) + 1)
                    p = probs[:, u.buf, w0 - n:w0]
                    nc.gpsimd.tensor_tensor(p, p, dec_r[:, WIN * P - n:], ALU.mult).then_inc(decayed, 1)

                def stage(i, q, heads):
                    nb = blocks(i)
                    kt = i + 1 - nb
                    vs, h = (vstage0, 0) if heads == 1 else (vstage, q * 3 + 1)
                    done = 0
                    while done < nb:
                        r = (kt + done) % VR
                        n = min(nb - done, VR - r)
                        src = vals[:, r:r + n, bass.ds(h * HD, heads * HD)].rearrange("p b (j d) -> p b j d", d=HD)
                        last = nc.gpsimd.tensor_copy(vs[:, done:done + n, :, 0:HD], src)
                        done += n
                    last.then_inc(staged, 1)

                def last_group(i):
                    pool.wait_ge(group_done, GROUPS * i + GROUPS - 1)
                    stage(i, GROUPS - 2, 3)

                def body(u, peeled):
                    if peeled == 0 and u.i > 0:
                        last_group(u.i - 1)
                    if peeled == 1:
                        if u.i % 2 == 0:
                            pool.wait_ge(vals_loaded[(u.i // 2) % 2], 16 * (u.i // 4 + 1))
                        stage(u.i, 0, 1)
                    if peeled is None and u.s == 1:
                        k = u.q - 1
                        pool.wait_ge(group_done, k + (GROUPS * u.i + 1))
                        stage(u.i, k, 3)
                    if u.by_act:
                        decay(u)

                for i in range(NT):
                    tile_units(pool, i, body)
                last_group(NT - 1)

            tsteps = [0]

            @block.vector
            def _(dve):
                dve.wait_ge(decay_loaded, 32)

                def serial(ins):
                    tsteps[0] += 1
                    ins.then_inc(t_step, 1)
                    dve.wait_ge(t_step, tsteps[0])

                def maximum(u, c):
                    k0, k1 = chunk_keys(u.i, c)
                    b = (chunk_base[u.i] + c + u.s * u.nc) % RING
                    dve.wait_ge(chunk_ready, u.chunk(c) + 1)
                    nc.vector.tensor_reduce(out=negmax[:, u.i % 2, u.h, c:c + 1], in_=s_ps[:, b, 0:k1 - k0],
                                            axis=AX_X, op=ALU.min).then_inc(max_ready, 1)

                def spreads(i):
                    n = chunks(i)
                    dve.wait_ge(max_ready, chunk_base[i + 1])
                    if i > first_multi:
                        dve.wait_ge(weight_ready, i - first_multi)
                    serial(nc.vector.tensor_reduce(out=negtop[:], in_=negmax[:, i % 2, :, 0:n], axis=AX_X, op=ALU.min))
                    nc.vector.tensor_tensor(spread[:, :, 0:n], negtop[:].unsqueeze(2).to_broadcast([P, NH, n]),
                                            negmax[:, i % 2, :, 0:n], ALU.subtract).then_inc(spread_ready, 1)

                def factors(i):
                    n = chunks(i)
                    dve.wait_ge(exp_done, chunk_base[i + 1])
                    if n == 1:
                        serial(nc.vector.reciprocal(factor[:], sums[:, i % 2, :, 0]))
                        return
                    dve.wait_ge(weight_ready, i + 1 - first_multi)
                    serial(nc.vector.tensor_tensor(scaled[:, :, 0:n], weight[:, :, 0:n], sums[:, i % 2, :, 0:n], ALU.mult))
                    serial(nc.vector.reduce_sum(total[:], scaled[:, :, 0:n], axis=AX_X))
                    serial(nc.vector.reciprocal(total[:], total[:]))
                    serial(nc.vector.tensor_tensor(factor[:], total[:], weight[:, :, 0], ALU.mult))

                def finish(i):
                    dve.wait_ge(back_ready, i + 1)
                    if i >= 2:
                        dve.wait_ge(y_stored[i % 2], 16 * (i // 2))
                    nc.vector.tensor_tensor(y_sb[:, i % 2, :].rearrange("p (h d) -> p h d", d=HD),
                                            t_ps[:, 0, :].rearrange("p (h w) -> p h w", w=TC)[:, :, 0:HD],
                                            factor[:].unsqueeze(2).to_broadcast([P, NH, HD]), ALU.mult).then_inc(y_out, 1)

                def group_to_sb(u):
                    n = u.q + u.i * GROUPS
                    dve.wait_ge(group_done, n + 1)
                    if u.i > 0 and isinstance(u.h, int) and u.h == 0:
                        dve.wait_ge(back_ready, u.i)
                    w = TC * len(group_heads(u))
                    nc.vector.tensor_copy(yT_sb[0:w, u.q, :], g_ps[0:w, 0:P]).then_inc(group_out, 1)

                def body(u, peeled):
                    t = u.back(TLAG)
                    maximum(u, 0)
                    if peeled == 2 and u.i > 0:
                        group_to_sb(Unit(u.i - 1, (NH - 1) // 3, 0))
                    if peeled == 3:
                        if u.i > 0:
                            finish(u.i - 1)
                        group_to_sb(Unit(u.i, 0, 0))
                    if peeled is None and u.s == 0:
                        group_to_sb(u.back(3))
                    evacuate(dve, t, 0, False)
                    if u.nc > 1:
                        maximum(u, 1)
                    evacuate(dve, t, 1, False)
                    for c in range(2, u.nc):
                        maximum(u, c)
                    if u.i > 0:
                        if peeled == 0 and chunks(u.i - 1) > 1:
                            spreads(u.i - 1)
                        if peeled == 1:
                            factors(u.i - 1)

                for i in range(NT):
                    tile_units(dve, i, body)
                end = Unit(NT - 1, NH // 3, NH % 3)
                for lag in range(TLAG, 0, -1):
                    for j in range(2):
                        evacuate(dve, end.back(lag), j, False)
                group_to_sb(Unit(NT - 1, (NH - 1) // 3, 0))
                spreads(NT - 1)
                factors(NT - 1)
                finish(NT - 1)

        B3 = 2
        NB = NT // B3
        xy_loaded = [sem(f"xy_loaded{b}") for b in range(2)]
        yT_ready = sem("yT_ready")
        yT_out = sem("yT_out")
        att_ready = sem("att_ready")
        x2_done = sem("x2_done")
        var_ready = sem("var_ready")
        dev_ready = sem("dev_ready")
        n_ready = sem("n_ready")
        nT_ready = sem("nT_ready")
        nT_out = sem("nT_out")
        ff_ready = sem("ff_ready")
        biased = sem("biased")
        o_ready = sem("o_ready")
        o_stored = [sem(f"o_stored{b}") for b in range(2)]
        r_step = sem("r_step")

        s3 = ExitStack()
        with s3:
            x_sb = sb("x_sb", [P, 2, B3, C], fp32, s3)
            yy = sb("yy", [P, 2, B3, C], fp32, s3)
            yT = sb("yT", [P, 2, B3, CH, P], fp32, s3)
            x2 = sb("x2", [P, 2, B3, C], fp32, s3)
            x2b = sb("x2b", [P, 2, B3, C], fp32, s3)
            nrm = sb("nrm", [P, 2, B3, C], fp32, s3)
            nT = sb("nT", [P, 2, B3, CH, P], fp32, s3)
            o_sb = sb("o_sb", [P, 2, B3, C], fp32, s3)
            q6 = sb("q6", [P, B3, 6], fp32, s3)
            mv3 = sb("mv3", [P, 2, B3, 2], fp32, s3)
            sd3 = sb("sd3", [P, 2, B3], fp32, s3)
            rs3 = sb("rs3", [P, 2, B3], fp32, s3)
            yT_ps = s3.enter_context(nc.psum_tensor("yT_ps", [P, 2, B3, CH, P], fp32))
            at_ps = s3.enter_context(nc.psum_tensor("at_ps", [P, 2, B3, C], fp32))
            nT_ps = s3.enter_context(nc.psum_tensor("nT_ps", [P, 2, B3, CH, P], fp32))
            ff_ps = s3.enter_context(nc.psum_tensor("ff_ps", [P, 2, B3, C], fp32))
            block = s3.enter_context(nc.Block())

            @block.sync
            def _(sp):
                def load(m):
                    sp.dma_start(yy[:, m % 2], y_tiles[:, B3 * m:B3 * (m + 1), :]).then_inc(xy_loaded[m % 2], 16)
                    sp.dma_start(x_sb[:, m % 2], x_tiles[:, B3 * m:B3 * (m + 1), :]).then_inc(xy_loaded[m % 2], 16)

                load(0)
                load(1)
                for m in range(NB):
                    if m + 2 < NB:
                        sp.wait_ge(x2_done, m + 1)
                        load(m + 2)
                    sp.wait_ge(o_ready, m + 1)
                    sp.dma_start(out_tiles[:, B3 * m:B3 * (m + 1), :], o_sb[:, m % 2]).then_inc(o_stored[m % 2], 16)
                for b in range(2):
                    sp.wait_ge(o_stored[b], 16 * (NB // 2))

            @block.tensor
            def _(pe):
                def half_a(m):
                    b = m % 2
                    pe.wait_ge(xy_loaded[b], 32 * (m // 2 + 1))
                    if m >= 2:
                        pe.wait_ge(yT_out, m - 1)
                    for t in range(B3):
                        for cc in range(CH):
                            last = nc.tensor.transpose(yT_ps[:, b, t, cc, :], yy[:, b, t, P * cc:P * (cc + 1)], ident[:])
                    last.then_inc(yT_ready, 1)
                    pe.wait_ge(yT_out, m + 1)
                    if m >= 2:
                        pe.wait_ge(x2_done, m - 1)
                    for t in range(B3):
                        for cc in range(CH):
                            last = nc.tensor.matmul(at_ps[:, b, t, :], yT[:, b, t, cc, :], wp_g[:, cc, :],
                                                    start=(cc == 0), stop=(cc == CH - 1))
                    last.then_inc(att_ready, 1)

                def half_b(m):
                    b = m % 2
                    pe.wait_ge(n_ready, m + 1)
                    if m >= 2:
                        pe.wait_ge(nT_out, m - 1)
                    for t in range(B3):
                        for cc in range(CH):
                            last = nc.tensor.transpose(nT_ps[:, b, t, cc, :], nrm[:, b, t, P * cc:P * (cc + 1)], ident[:])
                    last.then_inc(nT_ready, 1)
                    pe.wait_ge(nT_out, m + 1)
                    if m >= 2:
                        pe.wait_ge(o_ready, m - 1)
                    for t in range(B3):
                        for cc in range(CH):
                            last = nc.tensor.matmul(ff_ps[:, b, t, :], nT[:, b, t, cc, :], wf_g[:, cc, :],
                                                    start=(cc == 0), stop=(cc == CH - 1))
                    last.then_inc(ff_ready, 1)

                half_a(0)
                for m in range(NB):
                    if m + 1 < NB:
                        half_a(m + 1)
                    half_b(m)

            @block.scalar
            def _(act):
                def half_a(m):
                    b = m % 2
                    act.wait_ge(yT_ready, m + 1)
                    if m >= 2:
                        act.wait_ge(att_ready, m - 1)
                    nc.scalar.copy(yT[:, b], yT_ps[:, b]).then_inc(yT_out, 1)
                    act.wait_ge(var_ready, m + 1)
                    if m >= 2:
                        act.wait_ge(n_ready, m - 1)
                    nc.scalar.activation(sd3[:, b, :], mv3[:, b, :, 1], ACT.Sqrt, bias=eps_t[:, 0:1]).then_inc(dev_ready, 1)

                def half_b(m):
                    b = m % 2
                    act.wait_ge(nT_ready, m + 1)
                    if m >= 2:
                        act.wait_ge(ff_ready, m - 1)
                    nc.scalar.copy(nT[:, b], nT_ps[:, b]).then_inc(nT_out, 1)

                half_a(0)
                for m in range(NB):
                    if m + 1 < NB:
                        half_a(m + 1)
                    half_b(m)

            @block.gpsimd
            def _(pool):
                for m in range(NB):
                    b = m % 2
                    pool.wait_ge(x2_done, m + 1)
                    if m >= 2:
                        pool.wait_ge(o_ready, m - 1)
                    nc.gpsimd.tensor_tensor(x2b[:, b], x2[:, b], f_bias[:].unsqueeze(1).to_broadcast([P, B3, C]),
                                            ALU.add).then_inc(biased, 1)

            rsteps = [0]

            @block.vector
            def _(dve):
                def serial(ins):
                    rsteps[0] += 1
                    ins.then_inc(r_step, 1)
                    dve.wait_ge(r_step, rsteps[0])

                def half_a(m):
                    b = m % 2
                    dve.wait_ge(att_ready, m + 1)
                    dve.wait_ge(xy_loaded[b], 32 * (m // 2 + 1))
                    if m >= 2:
                        dve.wait_ge(biased, m - 1)
                    nc.vector.tensor_tensor(x2[:, b], x_sb[:, b], at_ps[:, b], ALU.add).then_inc(x2_done, 1)
                    dve.wait_ge(x2_done, m + 1)
                    for t in range(B3):
                        last = nc.vector.bn_stats(q6[:, t, :], x2[:, b, t, :])
                    serial(last)
                    for t in range(B3):
                        last = nc.vector.bn_aggr(mv3[:, b, t, :], q6[:, t, :])
                    last.then_inc(var_ready, 1)

                def half_a2(m):
                    b = m % 2
                    dve.wait_ge(dev_ready, m + 1)
                    serial(nc.vector.reciprocal(rs3[:, b, :], sd3[:, b, :]))
                    if m >= 2:
                        dve.wait_ge(nT_ready, m - 1)
                    dve.wait_ge(var_ready, m + 1)
                    for t in range(B3):
                        last = nc.vector.tensor_scalar(nrm[:, b, t, :], x2[:, b, t, :], mv3[:, b, t, 0:1], rs3[:, b, t:t + 1],
                                                       ALU.subtract, ALU.mult)
                    last.then_inc(n_ready, 1)

                def half_b(m):
                    b = m % 2
                    dve.wait_ge(ff_ready, m + 1)
                    dve.wait_ge(biased, m + 1)
                    if m >= 2:
                        dve.wait_ge(o_stored[b], 16 * (m // 2))
                    nc.vector.tensor_tensor(o_sb[:, b], ff_ps[:, b], x2b[:, b], ALU.add).then_inc(o_ready, 1)

                half_a(0)
                half_a2(0)
                for m in range(NB):
                    if m + 1 < NB:
                        half_a(m + 1)
                        half_a2(m + 1)
                    half_b(m)


def kernel(**inputs):
    import numpy as _np
    import concourse.bacc as _bacc
    from concourse import mybir as _mybir
    from concourse.bass_utils import run_bass_kernel_spmd as _run

    def a(name):
        return _np.asarray(inputs[name])

    P, WIN, LENGTH, ECHOIC = 128, 5, 512, 16
    ramp = _np.linspace(0.0, 1.0, LENGTH - ECHOIC + 1).astype(_np.float32)
    decay = 1.0 - _np.power(ramp, _np.float32(1.0 / _np.e))
    decay = _np.concatenate([_np.ones(ECHOIC - 1), decay]).astype(_np.float32)
    dist = _np.arange(P)[:, None] + P * (WIN - 1) - _np.arange(P * WIN)[None, :]
    rows = _np.where((dist >= 0) & (dist < LENGTH), decay[_np.clip(dist, 0, LENGTH - 1)], 0).astype(_np.float32)
    cols = rows.reshape(P, WIN, P).transpose(2, 1, 0)
    bf16 = _mybir.dt.np(_mybir.dt.bfloat16)
    causal = _np.where(_np.arange(P)[None, :] > _np.arange(P)[:, None], 1e30, 0.0).astype(bf16)

    ins = {
        "x": a("L0_attn_x")[0],
        "w_attn": a("L0_attn_W_attn"), "w_proj": a("L0_attn_W_proj"),
        "ffn_wT": a("L0_ffn_W").T, "ffn_b": a("L0_ffn_b")[None, :],
        "lora_downT": a("L0_ffn_lora_down").T, "lora_upT": a("L0_ffn_lora_up").T,
        "down_aux": a("L0_ffn_down_aux"), "up_auxT": a("L0_ffn_up_aux").T,
        "cond_cols": a("L0_c").reshape(2, P).T, "w_mod": a("L0_wmod"),
        "ident_in": _np.eye(P, dtype=_np.float32), "causal_in": causal, "decay_rows": rows, "decay_cols": cols,
    }
    nc = _bacc.Bacc("TRN2", target_bir_lowering=False, num_devices=1)
    arrays, args = {}, []
    for name, v in ins.items():
        v = _np.ascontiguousarray(v)
        arrays[f"{name}_dram"] = v
        args.append(nc.dram_tensor(f"{name}_dram", v.shape, _mybir.dt.from_np(v.dtype), kind="ExternalInput").ap())
    out = nc.dram_tensor("out_dram", ins["x"].shape, _mybir.dt.float32, kind="ExternalOutput").ap()
    bass_adaln_block_kernel(nc, *args, out)
    r = _run(nc, [arrays], core_ids=[0])
    return r.results[0]["out_dram"][None]
```

```python
import concourse.bass as bass
from concourse import mybir
from contextlib import ExitStack


def bass_adaln_block_kernel(nc, x, w_attn, w_proj, ffn_wT, ffn_b, lora_downT, lora_upT, down_aux, up_auxT,
                            cond_cols, w_mod, ident_in, causal_in, decay_cols, out):
    fp32 = mybir.dt.float32
    bf16 = mybir.dt.bfloat16
    ALU = mybir.AluOpType
    ACT = mybir.ActivationFunctionType
    AX_X = mybir.AxisListType.X

    P = 128
    T, C = x.shape
    CH = C // P
    NT = T // P
    NH, HD = 16, 16
    PARTS = 3
    PAIRS = [(0, 0), (0, 1), (0, 2), (1, 0), (1, 1), (2, 0)]
    SROWS = len(PAIRS) * HD
    G = 4
    GT = G * P
    NG = NT // G
    EPS = 1e-5
    BANK = 512
    CW = 2 * BANK
    RING = 3
    WIN = 5
    VR = 8
    SCORE_SCALE = -0.25
    SUM_LIMIT = 1e37

    def chunks(i):
        return -(-(i + 1) * P // CW)

    def newest(i):
        n = (i + 1) * P
        if chunks(i) in (2, 3):
            return max(P * WIN, n - CW * (chunks(i) - 1))
        return min(n, CW)

    def chunk_keys(i, c):
        n = (i + 1) * P
        if c == 0:
            return n - newest(i), n
        n -= newest(i)
        return max(0, n - CW * c), n - CW * (c - 1)

    def blocks(i):
        return min(WIN, i + 1)

    def jobs(i):
        nb = blocks(i)
        return [(0, min(3, nb))] + ([(3, nb)] if nb > 3 else [])

    NCMAX = chunks(NT - 1)
    first_multi = min(i for i in range(NT) if chunks(i) > 1)
    chunk_base = [0]
    for i in range(NT):
        chunk_base.append(chunk_base[-1] + NH * chunks(i))

    older_base = [0]
    for i in range(NT):
        older_base.append(older_base[-1] + NH * (chunks(i) - 1))

    jobs_base = [0]
    for i in range(NT):
        jobs_base.append(jobs_base[-1] + len(jobs(i)) * NH)

    class Unit:

        def __init__(self, i, q, s):
            self.i, self.q, self.s = i, q, s
            self.h = q * 3 + s
            self.nc = chunks(i)
            self.buf = (i * NH + s) % RING
            self.jobs = jobs(i)

        def chunk(self, c):
            return self.h * self.nc + (chunk_base[self.i] + c)

        def units(self):
            return self.h + self.i * NH

        def older(self, c):
            return self.h * (self.nc - 1) + (older_base[self.i] + c - 1)

        def place(self, c):
            if self.nc <= 2:
                return (self.i * NH + self.s - c) % RING
            return 0 if c == 0 else 1 + (c - 1) % 2

        def place_free(self, c):
            prev = self.back(1)
            if self.nc == 1:
                n = self.chunk(0) - (RING - 1)
                return None if isinstance(n, int) and n <= 0 else n
            if self.nc == 2:
                return prev.chunk(0) + c
            if c == 0:
                return prev.chunk(0) + 1
            if c <= 2:
                last = max(range(1, prev.nc), key=lambda k: (prev.nc > 2 and k % 2 == c % 2, k))
                return prev.chunk(last) + 1
            return self.chunk(c - 2) + 1

        def slot(self):
            return (self.s - 1) % 3

        def groups_before_reuse(self):
            if isinstance(self.h, int) and self.h < 2:
                return self.i * GROUPS
            return self.q + (self.i * GROUPS + 1 + (self.s - 1) // 3)

        def groups_issued(self):
            if isinstance(self.h, int) and self.h < 2:
                return self.i * GROUPS + self.h
            return self.q + (self.i * GROUPS + (self.s + 2) // 3)

        def all_jobs(self):
            return self.h * len(self.jobs) + jobs_base[self.i]

        def back(self, lag):
            if isinstance(self.q, int):
                h = self.h - lag
                i = self.i
                if h < 0:
                    h, i = h + NH, i - 1
                return Unit(i, h // 3, h % 3) if i >= 0 else None
            s = self.s - lag
            return Unit(self.i, self.q + s // 3, s % 3)

    PEEL = 4

    def tile_units(eng, i, body, straight):
        for h in range(PEEL):
            body(Unit(i, h // 3, h % 3), h)
        if straight:
            for h in range(PEEL, NH):
                body(Unit(i, h // 3, h % 3), None)
            return
        with eng.Fori(0, (NH - PEEL) // 3) as k:
            for r in range(3):
                s = PEEL + r
                body(Unit(i, k + s // 3, s % 3), None)

    TLAG = 2
    GROUPS = 1 + (NH - 1) // 3
    PULLERS = range(6, NH - 1, 3)
    SPLIT = 2

    def paired(eng, n, body):
        for g in (0, 1):
            body(g, g, 0, g, n - 1 - g)
        with eng.Fori(1, n // 2 - 1) as k:
            for b in range(2):
                body(k * 2 + b, b, k, 2, 2)
        for g in (n - 2, n - 1):
            body(g, g % 2, g // 2, 2, n - 1 - g)

    parts_d = nc.dram_tensor("parts_d", [PARTS, 2, C, T], bf16, kind="Internal").ap()
    v_d = nc.dram_tensor("v_d", [T, C], fp32, kind="Internal").ap()
    y_d = nc.dram_tensor("y_d", [T, C], fp32, kind="Internal").ap()
    x_tiles = x.rearrange("(t p) c -> p t c", p=P)
    v_tiles = v_d.rearrange("(t p) c -> p t c", p=P)
    y_tiles = y_d.rearrange("(t p) c -> p t c", p=P)
    out_tiles = out.rearrange("(t p) c -> p t c", p=P)

    ctx = ExitStack()
    with ctx:
        def sb(name, shape, dt, scope=ctx):
            return scope.enter_context(nc.sbuf_tensor(name, shape, dt))

        def sem(name):
            return ctx.enter_context(nc.semaphore(name))

        k_stack = sb("k_stack", [SROWS, NH, T], bf16)
        ident = sb("ident", [P, P], fp32)
        ident_b = sb("ident_b", [P, P], bf16)
        causal = sb("causal", [P, P], bf16)
        wp_g = sb("wp_g", [P, CH, C], fp32)
        wf_g = sb("wf_g", [P, CH, C], fp32)
        f_bias = sb("f_bias", [P, C], fp32)
        eps_t = sb("eps_t", [P, 1], fp32)

        cond_loaded = sem("cond_loaded")
        wm_loaded = sem("wm_loaded")
        wa_loaded = sem("wa_loaded")
        aux_loaded = sem("aux_loaded")
        x_loaded = [sem(f"x_loaded{b}") for b in range(2)]
        v_step = sem("v_step")
        a_step = sem("a_step")
        pe_step = sem("pe_step")
        stat6_done = sem("stat6_done")
        stats_ready = sem("stats_ready")
        std_ready = sem("std_ready")
        rstd_done = sem("rstd_done")
        xn_ready = sem("xn_ready")
        xnT_ready = sem("xnT_ready")
        hT_by_act = sem("hT_by_act")
        hT_by_dve = sem("hT_by_dve")
        kq_ready = sem("kq_ready")
        v_ready = sem("v_ready")
        kq_out = sem("kq_out")
        v_out = sem("v_out")
        high_ready = sem("high_ready")
        rest1_ready = sem("rest1_ready")
        mid_ready = sem("mid_ready")
        low_ready = sem("low_ready")
        part_stored = [[sem(f"{name}_stored{b}") for b in range(2)] for name in ("high", "mid", "low")]
        v_stored = [sem(f"v_stored{b}") for b in range(2)]
        k_loaded = sem("k_loaded")
        k_last = sem("k_last")

        s1 = ExitStack()
        with s1:
            w0 = sb("w0", [P, 9 * CH * C], fp32, s1)
            wmod_t = w0[:, 0:6 * CH * C].rearrange("p (h n) -> p h n", h=CH)
            wa = w0[:, 6 * CH * C:].rearrange("p (h n) -> p h n", h=CH)
            wa_f = w0[:, 0:3 * CH * C].rearrange("p (h n) -> p h n", h=CH)
            hT_odd = w0[:, 3 * CH * C:3 * CH * C + CH * GT].rearrange("p (h t) -> p h t", h=CH)
            v_sb = w0[:, 6 * CH * C:6 * CH * C + G * C].rearrange("p (t c) -> p t c", t=G)
            ld_t = sb("ld_t", [100, 4], fp32, s1)
            lu_t = sb("lu_t", [4, 50], fp32, s1)
            da_t = sb("da_t", [100, C], fp32, s1)
            ua_t = sb("ua_t", [50, C], fp32, s1)
            b_row = sb("b_row", [1, C], fp32, s1)
            ones_t = sb("ones_t", [P, P], fp32, s1)
            cnd = sb("cnd", [P, CH], fp32, s1)
            sil = sb("sil", [P, CH], fp32, s1)
            tmp_c = sb("tmp_c", [P, CH], fp32, s1)
            kq32 = sb("kq32", [P, 2, 4, GT], fp32, s1)
            sil_bc = kq32[:, 0, 0, 0:CH * P].rearrange("p (h n) -> p h n", h=CH)
            sh_a = kq32[:, 0, 1, 0:CH * P].rearrange("p (h n) -> p h n", h=CH)
            mod_c = sb("mod_c", [P, 4, CH], fp32, s1)
            gates = sb("gates", [P, 2, C], fp32, s1)
            kq_bias = sb("kq_bias", [P, 4], fp32, s1)
            v_bias = sb("v_bias", [P, C], fp32, s1)
            a2_t = sb("a2_t", [4, C], fp32, s1)
            a3_t = sb("a3_t", [50, C], fp32, s1)
            xs = sb("xs", [P, 2, G, C], fp32, s1)
            sh_b = xs[:, 0, 0, :].rearrange("p (h n) -> p h n", h=CH)
            gsign = xs[:, 0, 2:4, :]
            xn = sb("xn", [P, G, C], fp32, s1)
            st6 = sb("st6", [P, 2, G, 6], fp32, s1)
            mv = sb("mv", [P, 2, G, 2], fp32, s1)
            sd = sb("sd", [P, 2, G], fp32, s1)
            rsd = sb("rsd", [P, 2, G], fp32, s1)
            hT = [sb("hT", [P, CH, GT], fp32, s1)[:], hT_odd]
            part = [sb(f"part{n}", [P, 4, GT], bf16, s1) for n in range(PARTS)]
            pt_ps = s1.enter_context(nc.psum_tensor("pt_ps", [P, CH, GT], fp32))
            kq_ps = s1.enter_context(nc.psum_tensor("kq_ps", [P, 4, GT], fp32))
            v_ps = s1.enter_context(nc.psum_tensor("v_ps", [P, G, C], fp32))
            w_ps = kq_ps

            KQ_OFF = [C, C + P, 0, P]
            SHIFT_A, SCALE_A, SHIFT_B, SCALE_B = range(4)
            MOD_OF = [0, 1, 3, 4]

            wa_d = w_attn.rearrange("(h p) n -> p h n", p=P)
            PE_MOD, PE_GATES, PE_BIAS, PE_A2, PE_A3, PE_LW, PE_FB = range(1, 8)
            V_EPS, V_SIL, V_SH, V_BIAS, V_A2, V_A3, V_WF = 2, 7, 10, 20, 21, 22, 30

            block = s1.enter_context(nc.Block())

            @block.sync
            def _(sp):
                sp.dma_start(cnd[:], cond_cols).then_inc(cond_loaded, 16)
                sp.dma_start(wmod_t, w_mod.rearrange("(h p) n -> p h n", p=P)).then_inc(wm_loaded, 16)

                def load_x(g, b):
                    sp.dma_start(xs[:, b], x_tiles[:, bass.ds(g * G, G), :]).then_inc(x_loaded[b], 16)

                load_x(0, 0)
                for dst, src in ((ident[:], ident_in), (wa, wa_d)):
                    sp.dma_start(dst, src).then_inc(wa_loaded, 16)
                load_x(1, 1)
                for dst, src in ((wp_g[:], w_proj.rearrange("(h p) n -> p h n", p=P)),
                                 (wf_g[:], ffn_wT.rearrange("(h p) n -> p h n", p=P)),
                                 (ld_t[:], lora_downT), (lu_t[:], lora_upT), (da_t[:], down_aux),
                                 (ua_t[:], up_auxT), (b_row[:], ffn_b), (causal[:], causal_in)):
                    sp.dma_start(dst, src).then_inc(aux_loaded, 16)

                sp.wait_ge(xn_ready, 1)
                load_x(2, 0)

                def body(g, b, k, first, last):
                    tok = bass.ds(g * GT, GT)
                    if g + 3 < NG:
                        sp.wait_ge(xn_ready, g + 2)
                        load_x(g + 3, 1 - b)
                    for n, ready in ((0, high_ready), (None, v_out), (1, mid_ready), (2, low_ready)):
                        sp.wait_ge(ready, g + 1)
                        if n == 2 and g == NG - 1:
                            sp.wait_ge(low_ready, NG + 1)
                        if n is None:
                            sp.dma_start(v_tiles[:, bass.ds(g * G, G), :], v_sb).then_inc(v_stored[b], 16)
                            if g > 0:
                                stack_keys(g - 1)
                            continue
                        for kq in range(2):
                            sp.dma_start(parts_d[n, kq].rearrange("(m p) t -> p m t", p=P)[:, :, tok],
                                         part[n][:, 2 * kq:2 * kq + 2, :]).then_inc(part_stored[n][b], 16)

                def stack_keys(g):
                    for n in range(PARTS):
                        sp.wait_ge(part_stored[n][g % 2], (g // 2 + 1) * 32)
                    for j, (_, kp) in enumerate(PAIRS):
                        sp.dma_start(k_stack[HD * j:HD * (j + 1), :, g * GT:(g + 1) * GT],
                                     parts_d[kp, 0, :, g * GT:(g + 1) * GT].rearrange("(h d) t -> d h t", d=HD)
                                     ).then_inc(k_loaded if g < NG - 1 else k_last, 16)

                for g in range(NG):
                    body(g, g % 2, g // 2, min(g, 2), min(NG - 1 - g, 2))
                stack_keys(NG - 1)
                sp.wait_ge(k_loaded, 16 * len(PAIRS) * (NG - 1))
                for b in range(2):
                    sp.wait_ge(v_stored[b], 16 * (NG // 2))

            @block.scalar
            def _(act):
                act.wait_ge(cond_loaded, 16)
                nc.scalar.activation(tmp_c[:], cnd[:], ACT.Exp, scale=-1.0).then_inc(a_step, 1)
                act.wait_ge(v_step, V_EPS)

                def std(g, b):
                    act.wait_ge(stats_ready, g + 1)
                    nc.scalar.activation(sd[:, b, :], mv[:, b, :, 1], ACT.Sqrt, bias=eps_t[:, 0:1]).then_inc(std_ready, 1)

                def half_hT(g, b):
                    act.wait_ge(xnT_ready, g + 1)
                    nc.scalar.copy(hT[b][:, 0, :], pt_ps[:, 0, :]).then_inc(hT_by_act, 1)

                std(0, 0)
                half_hT(0, 0)
                std(1, 1)

                def body(g, b, k, first, last):
                    if first >= 2:
                        act.wait_ge(low_ready, g - 1)
                    elif first == 0:
                        act.wait_ge(v_step, V_BIAS)
                    for m in range(4):
                        act.wait_ge(kq_ready, g * 4 + (m + 1))
                        nc.scalar.activation(kq32[:, b, m, :], kq_ps[:, m, :], ACT.Identity, bias=kq_bias[:, m:m + 1]
                                             ).then_inc(kq_out, 1)
                    if last >= 1:
                        if first >= 1:
                            act.wait_ge(v_ready, g)
                        half_hT(g + 1, 1 - b)
                    if first >= 1:
                        act.wait_ge(part_stored[0][1 - b], (k + b) * 32)
                    act.wait_ge(kq_out, g * 4 + 4)
                    nc.scalar.copy(part[0][:], kq32[:, b]).then_inc(high_ready, 1)
                    if last >= 2:
                        std(g + 2, b)
                    act.wait_ge(rest1_ready, g + 1)
                    if first >= 1:
                        act.wait_ge(part_stored[1][1 - b], (k + b) * 32)
                        act.wait_ge(low_ready, g)
                    nc.scalar.copy(part[1][:], kq32[:, b]).then_inc(mid_ready, 1)

                paired(act, NG, body)

            @block.gpsimd
            def _(pool):
                def body(g, b, k, first, last):
                    pool.wait_ge(mid_ready, g + 1)
                    if first >= 1:
                        pool.wait_ge(part_stored[2][1 - b], (k + b) * 32)
                    n = 4 if last >= 1 else 2
                    nc.gpsimd.tensor_tensor(part[2][:, 0:n, :], kq32[:, b, 0:n, :], part[1][:, 0:n, :], ALU.subtract
                                            ).then_inc(low_ready, 1)

                paired(pool, NG, body)

            steps = [0]

            @block.vector
            def _(dve):
                def step(ins):
                    steps[0] += 1
                    ins.then_inc(v_step, 1)
                    return steps[0]

                def serial(ins):
                    dve.wait_ge(v_step, step(ins))

                step(nc.vector.memset(ones_t[:], 1.0))
                serial(nc.vector.memset(eps_t[:], EPS))
                assert steps[0] == V_EPS
                dve.wait_ge(a_step, 1)
                serial(nc.vector.tensor_scalar_add(tmp_c[:], tmp_c[:], 1.0))
                serial(nc.vector.reciprocal(tmp_c[:], tmp_c[:]))
                serial(nc.vector.tensor_tensor(sil[:], cnd[:], tmp_c[:], ALU.mult))
                for cc in range(CH):
                    n = step(nc.vector.tensor_scalar(sil_bc[:, cc, :], ones_t[:], sil[:, cc:cc + 1], None, ALU.mult))
                assert n == V_SIL
                def stats(g, b, k):
                    dve.wait_ge(x_loaded[b], (k + 1) * 16)
                    for t in range(G):
                        last = nc.vector.bn_stats(st6[:, b, t, :], xs[:, b, t, :])
                    last.then_inc(stat6_done, 1)

                def means(g, b):
                    for t in range(G):
                        last = nc.vector.bn_aggr(mv[:, b, t, :], st6[:, b, t, :])
                    last.then_inc(stats_ready, 1)

                def normalise(g, b):
                    dve.wait_ge(std_ready, g + 1)
                    nc.vector.reciprocal(rsd[:, b, :], sd[:, b, :]).then_inc(rstd_done, 1)
                    dve.wait_ge(rstd_done, g + 1)
                    for t in range(G):
                        last = nc.vector.tensor_scalar(xn[:, t, :], xs[:, b, t, :], mv[:, b, t, 0:1],
                                                       rsd[:, b, t:t + 1], ALU.subtract, ALU.mult)
                    last.then_inc(xn_ready, 1)

                def half_hT(g, b):
                    dve.wait_ge(xnT_ready, g + 1)
                    nc.vector.tensor_copy(hT[b][:, 1, :], pt_ps[:, 1, :]).then_inc(hT_by_dve, 1)

                stats(0, 0, 0)
                dve.wait_ge(stat6_done, 1)
                means(0, 0)
                dve.wait_ge(stats_ready, 1)
                normalise(0, 0)
                dve.wait_ge(pe_step, PE_MOD)
                serial(nc.vector.tensor_copy(mod_c[:], w_ps[:, 2, 0:8].rearrange("p (v h) -> p v h", h=CH)))
                for cc in range(CH):
                    n = step(nc.vector.tensor_scalar(sh_a[:, cc, :], ones_t[:], mod_c[:, SHIFT_A, cc:cc + 1], None, ALU.mult))
                assert n == V_SH
                for v in (SCALE_A, SCALE_B):
                    serial(nc.vector.tensor_scalar_add(mod_c[:, v, :], mod_c[:, v, :], 1.0))
                dve.wait_ge(pe_step, PE_GATES)
                step(nc.vector.tensor_copy(gates[:].rearrange("p a c -> p (a c)"), w_ps[:, 0, :]))
                dve.wait_ge(wa_loaded, 32)
                for cc in range(CH):
                    step(nc.vector.tensor_scalar(wa_f[:, cc, 0:C], wa[:, cc, 0:C], mod_c[:, SCALE_A, cc:cc + 1],
                                                 SCORE_SCALE, ALU.mult, ALU.mult))
                    step(nc.vector.tensor_scalar(wa_f[:, cc, C:3 * C], wa[:, cc, C:3 * C],
                                                 mod_c[:, SCALE_A, cc:cc + 1], None, ALU.mult))
                half_hT(0, 0)
                stats(1, 1, 0)
                dve.wait_ge(stat6_done, 2)
                means(1, 1)
                dve.wait_ge(pe_step, PE_BIAS)
                step(nc.vector.tensor_copy(kq_bias[:, 0:2], w_ps[:, 2, 0:2]))
                step(nc.vector.tensor_scalar(kq_bias[:, 2:4], w_ps[:, 2, 2:4], SCORE_SCALE, None, ALU.mult))
                serial(nc.vector.tensor_copy(v_bias[:], w_ps[:, 1, 0:C]))
                assert steps[0] == V_BIAS

                def body(g, b, k, first, last):
                    if last >= 1:
                        dve.wait_ge(xnT_ready, g + 1)
                        dve.wait_ge(stats_ready, g + 2)
                        normalise(g + 1, 1 - b)
                    if last >= 2:
                        stats(g + 2, b, k + 1)
                    if last >= 1:
                        if first >= 1:
                            dve.wait_ge(v_ready, g)
                        if last >= 2:
                            dve.wait_ge(stat6_done, g + 3)
                        half_hT(g + 1, 1 - b)
                    if last >= 2:
                        means(g + 2, b)
                    dve.wait_ge(high_ready, g + 1)
                    nc.vector.tensor_tensor(kq32[:, b], kq32[:, b], part[0][:], ALU.subtract).then_inc(rest1_ready, 1)
                    dve.wait_ge(v_ready, g + 1)
                    if first >= 1:
                        dve.wait_ge(v_stored[1 - b], (k + b) * 16)
                    nc.vector.tensor_tensor(v_sb, v_ps[:], v_bias[:].unsqueeze(1).to_broadcast([P, G, C]),
                                            ALU.add).then_inc(v_out, 1)
                    if last == 0:
                        dve.wait_ge(mid_ready, NG)
                        dve.wait_ge(low_ready, NG - 1)
                        dve.wait_ge(part_stored[2][1 - b], (k + b) * 32)
                        nc.vector.tensor_tensor(part[2][:, 2:4, :], kq32[:, b, 2:4, :], part[1][:, 2:4, :], ALU.subtract
                                                ).then_inc(low_ready, 1)

                paired(dve, NG, body)

                dve.wait_ge(pe_step, PE_A2)
                assert step(nc.vector.tensor_copy(a2_t[:], w_ps[0:4, 3, 0:C])) == V_A2
                dve.wait_ge(pe_step, PE_A3)
                assert step(nc.vector.tensor_copy(a3_t[:], w_ps[0:50, 3, 0:C])) == V_A3
                g2 = gates[:].rearrange("p a c -> p (a c)")
                s2 = gsign.rearrange("p a c -> p (a c)")
                serial(nc.vector.tensor_scalar(s2, g2, 0.0, 2.0, ALU.is_ge, ALU.mult))
                serial(nc.vector.tensor_scalar_add(s2, s2, -1.0))
                serial(nc.vector.tensor_tensor(g2, g2, s2, ALU.mult))
                serial(nc.vector.scalar_tensor_tensor(g2, g2, 0.25, s2, ALU.max, ALU.mult))
                for cc in range(CH):
                    step(nc.vector.tensor_scalar(sh_b[:, cc, :], ones_t[:], mod_c[:, SHIFT_B, cc:cc + 1], None, ALU.mult))
                dve.wait_ge(pe_step, PE_LW)
                for cc in range(CH):
                    serial(nc.vector.tensor_tensor(wf_g[:, cc, :], wf_g[:, cc, :], w_ps[:, 3, C * cc:C * (cc + 1)], ALU.add))
                assert steps[0] == V_WF
                dve.wait_ge(pe_step, PE_FB)
                for cc in range(CH):
                    step(nc.vector.tensor_tensor(wp_g[:, cc, :], wp_g[:, cc, :], gates[:, 0, :], ALU.mult))
                    step(nc.vector.scalar_tensor_tensor(wf_g[:, cc, :], wf_g[:, cc, :], mod_c[:, SCALE_B, cc:cc + 1],
                                                        gates[:, 1, :], ALU.mult, ALU.mult))
                step(nc.vector.tensor_tensor(f_bias[:], w_ps[:, 0, 0:C], gates[:, 1, :], ALU.mult))
                serial(nc.vector.tensor_copy(ident_b[:], ident[:]))

            @block.tensor
            def _(pe):
                def transposes(g):
                    pe.wait_ge(xn_ready, g + 1)
                    for t in range(G):
                        for cc in range(CH):
                            last = nc.tensor.transpose(pt_ps[:, cc, P * t:P * (t + 1)], xn[:, t, P * cc:P * (cc + 1)], ident[:])
                    last.then_inc(xnT_ready, 1)

                pe.wait_ge(wm_loaded, 16)
                pe.wait_ge(v_step, V_SIL)
                for a, v in enumerate(MOD_OF):
                    for hf in range(CH):
                        for cc in range(CH):
                            last = nc.tensor.matmul(w_ps[:, 2, 2 * a + hf:2 * a + hf + 1],
                                                    wmod_t[:, cc, C * v + P * hf:C * v + P * (hf + 1)],
                                                    sil[:, cc:cc + 1], start=(cc == 0), stop=(cc == CH - 1))
                last.then_inc(pe_step, 1)
                for a, v in ((0, 2), (1, 5)):
                    for cc in range(CH):
                        last = nc.tensor.matmul(w_ps[:, 0, C * a:C * (a + 1)], sil_bc[:, cc, :],
                                                wmod_t[:, cc, C * v:C * (v + 1)], start=(cc == 0), stop=(cc == CH - 1))
                last.then_inc(pe_step, 1)
                pe.wait_ge(wa_loaded, 32)
                transposes(0)
                pe.wait_ge(v_step, V_SH)
                for m in range(4):
                    for cc in range(CH):
                        nc.tensor.matmul(w_ps[:, 2, m:m + 1], wa[:, cc, KQ_OFF[m]:KQ_OFF[m] + P],
                                         mod_c[:, SHIFT_A, cc:cc + 1], start=(cc == 0), stop=(cc == CH - 1))
                for cc in range(CH):
                    last = nc.tensor.matmul(w_ps[:, 1, 0:C], sh_a[:, cc, :], wa[:, cc, 2 * C:3 * C],
                                            start=(cc == 0), stop=(cc == CH - 1))
                last.then_inc(pe_step, 1)
                pe.wait_ge(v_step, V_BIAS)

                def body(g, b, k, first, last):
                    pe.wait_ge(hT_by_act, g + 1)
                    pe.wait_ge(hT_by_dve, g + 1)
                    for m in range(4):
                        if first >= 1:
                            pe.wait_ge(kq_out, g * 4 + (m - 3))
                        for cc in range(CH):
                            mm = nc.tensor.matmul(kq_ps[:, m, :], wa_f[:, cc, KQ_OFF[m]:KQ_OFF[m] + P], hT[b][:, cc, :],
                                                  start=(cc == 0), stop=(cc == CH - 1))
                        mm.then_inc(kq_ready, 1)
                    if last >= 1:
                        transposes(g + 1)
                    if first >= 1:
                        pe.wait_ge(v_out, g)
                    for t in range(G):
                        for cc in range(CH):
                            mm = nc.tensor.matmul(v_ps[:, t, :], hT[b][:, cc, P * t:P * (t + 1)], wa_f[:, cc, 2 * C:3 * C],
                                                  start=(cc == 0), stop=(cc == CH - 1))
                    mm.then_inc(v_ready, 1)

                paired(pe, NG, body)

                pe.wait_ge(kq_out, 4 * NG)
                pe.wait_ge(aux_loaded, 128)
                nc.tensor.matmul(w_ps[0:4, 3, 0:C], ld_t[:], da_t[:], start=True, stop=True).then_inc(pe_step, 1)
                pe.wait_ge(v_step, V_A2)
                nc.tensor.matmul(w_ps[0:50, 3, 0:C], lu_t[:], a2_t[:], start=True, stop=True).then_inc(pe_step, 1)
                pe.wait_ge(v_step, V_A3)
                for cc in range(CH):
                    last = nc.tensor.matmul(w_ps[:, 3, C * cc:C * (cc + 1)], a3_t[:, P * cc:P * (cc + 1)], ua_t[:],
                                            start=True, stop=True)
                last.then_inc(pe_step, 1)
                pe.wait_ge(v_step, V_WF)
                for cc in range(CH):
                    nc.tensor.matmul(w_ps[:, 0, 0:C], sh_b[:, cc, :], wf_g[:, cc, :], start=(cc == 0), stop=False)
                nc.tensor.matmul(w_ps[:, 0, 0:C], ones_t[0:1, :], b_row[:], start=False, stop=True).then_inc(pe_step, 1)

        redo = sb("redo", [1, 1], mybir.dt.int32)

        def attention(full):
            tag = "full_" if full else "fast_"
            s2 = ExitStack()
            q_loaded = [sem(tag + f"q_loaded{b}") for b in range(2)]
            vals_loaded = [sem(tag + f"vals_loaded{b}") for b in range(2)]
            decay_loaded = sem(tag + "decay_loaded")
            head_ready = sem(tag + "head_ready")
            older_ready = sem(tag + "older_ready")
            max_ready = sem(tag + "max_ready")
            exp_done = sem(tag + "exp_done")
            job_ready = sem(tag + "job_ready")
            job_out = sem(tag + "job_out")
            staged = sem(tag + "staged")
            group_done = sem(tag + "group_done")
            group_out = sem(tag + "group_out")
            back_ready = sem(tag + "back_ready")
            spread_ready = sem(tag + "spread_ready")
            weight_ready = sem(tag + "weight_ready")
            y_out = sem(tag + "y_out")
            y_stored = [sem(tag + f"y_stored{b}") for b in range(2)]
            t_step = sem(tag + "t_step")
            zeroed = sem(tag + "zeroed")

            worst_ready = sem(tag + "worst_ready")
            worst_steps = 2 + 3 * NT

            with s2:
                q_stack = sb(tag + "q_stack", [SROWS, 2, NH, 2 * P], bf16, s2)
                probs = sb(tag + "probs", [P, RING, CW], fp32, s2)
                probsT = sb(tag + "probsT", [P, RING, WIN, P], fp32, s2)
                vals = sb(tag + "vals", [P, VR, C], fp32, s2)
                dec_c = sb(tag + "dec_c", [P, WIN, P], fp32, s2)
                worst = sb(tag + "worst", [P, NH], fp32, s2)
                worst_row = sb(tag + "worst_row", [P, 1], fp32, s2)
                TC = 32
                vstage0 = sb(tag + "vstage0", [P, WIN, 1, TC], fp32, s2)
                vstage = sb(tag + "vstage", [P, WIN, 3, TC], fp32, s2)
                yT_sb = sb(tag + "yT_sb", [3 * TC, GROUPS, P], fp32, s2)
                y_sb = sb(tag + "y_sb", [P, 2, C], fp32, s2)
                negmax = sb(tag + "negmax", [P, 2, NH, NCMAX], fp32, s2)
                sums = sb(tag + "sums", [P, 2, NH, NCMAX], fp32, s2)
                negtop = sb(tag + "negtop", [P, NH], fp32, s2)
                spread = sb(tag + "spread", [P, NH, NCMAX], fp32, s2)
                weight = sb(tag + "weight", [P, NH, NCMAX], fp32, s2)
                scaled = sb(tag + "scaled", [P, NH, NCMAX], fp32, s2)
                total = sb(tag + "total", [P, NH], fp32, s2)
                factor = sb(tag + "factor", [P, NH], fp32, s2)
                s_ps = s2.enter_context(nc.psum_tensor(tag + "s_ps", [P, RING, CW], fp32))
                t_ps = s2.enter_context(nc.psum_tensor(tag + "t_ps", [P, 2, BANK], fp32))
                g_ps = t_ps[:, 1, :]
                block = s2.enter_context(nc.Block())

                @block.sync
                def _(sp):
                    def store_y(i):
                        sp.wait_ge(y_out, i + 1)
                        sp.dma_start(y_tiles[:, i, :], y_sb[:, i % 2, :]).then_inc(y_stored[i % 2], 16)

                    for m in range(NT // 2):
                        if m >= 2:
                            sp.wait_ge(head_ready, NH * (2 * m - 2))
                            if older_base[2 * m - 2] > 0:
                                sp.wait_ge(older_ready, older_base[2 * m - 2])
                        for j, (qp, _) in enumerate(PAIRS):
                            sp.dma_start(q_stack[HD * j:HD * (j + 1), m % 2, :, :],
                                         parts_d[qp, 1, :, 2 * P * m:2 * P * (m + 1)].rearrange("(h d) t -> d h t", d=HD)
                                         ).then_inc(q_loaded[m % 2], 16)
                        if m == 0:
                            sp.dma_start(dec_c[:], decay_cols).then_inc(decay_loaded, 16)
                        if m >= VR // 2:
                            sp.wait_ge(staged, GROUPS * (2 * m - VR + WIN + 1))
                        sp.dma_start(vals[:, (2 * m) % VR:(2 * m) % VR + 2, :], v_tiles[:, 2 * m:2 * m + 2, :]
                                     ).then_inc(vals_loaded[m % 2], 16)
                        for i in (2 * m - 4, 2 * m - 3):
                            if i >= 0:
                                store_y(i)
                    for i in range(NT - 4, NT):
                        store_y(i)
                    for b in range(2):
                        sp.wait_ge(y_stored[b], 16 * (NT // 2))

                def pulls(u):
                    return not full and u is not None and u.nc == 1 and u.h in PULLERS

                def following(u):
                    return Unit(u.i, (u.h + 1) // 3, (u.h + 1) % 3)

                def score_chunk(pe, u, c):
                    k0, k1 = chunk_keys(u.i, c)
                    b = u.place(c)
                    need = u.place_free(c)
                    if need is not None:
                        pe.wait_ge(exp_done, need)
                    q = q_stack[:, (u.i // 2) % 2, u.h, P * (u.i % 2):P * (u.i % 2 + 1)]
                    for o in range(0, k1 - k0, BANK):
                        n = min(BANK, k1 - k0 - o)
                        diag = c == 0 and k0 + o + n == k1
                        last = nc.tensor.matmul(s_ps[:, b, o:o + n], q, k_stack[:, u.h, k0 + o:k0 + o + n],
                                                start=True, stop=not diag)
                        if diag:
                            last = nc.tensor.matmul(s_ps[:, b, o + n - P:o + n], ident_b[:], causal[:], start=False, stop=True)
                    last.then_inc(head_ready if c == 0 else older_ready, 1)

                def transpose_job(pe, u, j):
                    if j == 0:
                        pe.wait_ge(exp_done, u.chunk(0) + 1)
                    prev = u.back(1)
                    if prev is not None and j < len(prev.jobs):
                        pe.wait_ge(job_out, prev.all_jobs() + (j + 1))
                    if j == 0 and isinstance(u.h, int) and u.h == 1 and u.i > 0:
                        pe.wait_ge(y_out, u.i)
                    if j == 1:
                        pe.wait_ge(group_out, u.groups_issued())
                    w0 = newest(u.i)
                    b0, b1 = u.jobs[j]
                    for b in range(b0, b1):
                        lo = w0 - P * (blocks(u.i) - b)
                        last = nc.tensor.transpose(t_ps[:, j, P * (b - b0):P * (b - b0 + 1)], probs[:, u.buf, lo:lo + P], ident[:])
                    last.then_inc(job_ready, 1)

                def group_heads(u):
                    return [u] if isinstance(u.h, int) and u.h == 0 else [u.back(2), u.back(1), u]

                def values_group(pe, u, b0=0, b1=WIN):
                    n = u.q + u.i * GROUPS
                    if b0 == 0:
                        after = Unit(u.i, u.q, u.s + 1)
                        pe.wait_ge(job_out, after.all_jobs())
                        pe.wait_ge(staged, n + 1)
                        if not (isinstance(n, int) and n == 0):
                            pe.wait_ge(group_out, n)
                    heads = group_heads(u)
                    vs = vstage0 if len(heads) == 1 else vstage
                    nb = blocks(u.i)
                    for b in range(b0, min(b1, nb)):
                        for j, v in enumerate(heads):
                            last = nc.tensor.matmul(g_ps[TC * j:TC * (j + 1), 0:P], vs[:, b, j, :],
                                                    probsT[:, v.slot(), b, :], start=(b == 0), stop=(b == nb - 1))
                    if b1 >= nb:
                        last.then_inc(group_done, 1)

                def turn_back(pe, i):
                    last_t = Unit(i + 1, 0, 0) if i + 1 < NT else Unit(i, (NH - 1) // 3, (NH - 1) % 3)
                    pe.wait_ge(job_out, last_t.all_jobs() + 1)
                    pe.wait_ge(group_out, GROUPS * (i + 1))
                    for g in range(GROUPS):
                        w = TC if g == 0 else 3 * TC
                        o = 0 if g == 0 else TC + 3 * TC * (g - 1)
                        last = nc.tensor.transpose(t_ps[:, 0, o:o + w], yT_sb[0:w, g, :], ident[0:w, 0:w])
                    last.then_inc(back_ready, 1)

                @block.tensor
                def _(pe):
                    def body(u, peeled):
                        t = u.back(TLAG)
                        if peeled == 0 and u.i % 2 == 0:
                            pe.wait_ge(q_loaded[(u.i // 2) % 2], 96 * (u.i // 4 + 1))
                        if peeled == 0 and u.i == NT - G:
                            pe.wait_ge(k_last, 16 * len(PAIRS))
                        prev = u.back(1)
                        older = list(range(1, prev.nc)) if prev is not None else []
                        for c in older[0:2]:
                            score_chunk(pe, prev, c)
                        if peeled == 2 and u.i > 0:
                            group = Unit(u.i - 1, (NH - 1) // 3, 0)
                        elif peeled == 3:
                            group = Unit(u.i, 0, 0)
                        else:
                            group = u.back(3) if peeled is None and u.s == 0 else None
                        early = group is not None and peeled != 3 and prev.nc > 2
                        before = group is None and prev is not None and prev.nc == 3
                        if early:
                            values_group(pe, group, 0, SPLIT)
                        if before:
                            transpose_job(pe, t, 0)
                        if not pulls(prev):
                            score_chunk(pe, u, 0)
                        if pulls(u):
                            score_chunk(pe, following(u), 0)
                        if peeled == 3 and u.i > 0:
                            turn_back(pe, u.i - 1)
                        if group is not None and not early:
                            values_group(pe, group)
                        for c in older[2:]:
                            score_chunk(pe, prev, c)
                        if early:
                            values_group(pe, group, SPLIT)
                        if t is not None and not before:
                            transpose_job(pe, t, 0)
                        if t is not None and len(t.jobs) > 1:
                            transpose_job(pe, t, 1)

                    for i in range(NT):
                        tile_units(pe, i, body, not full)
                    for c in range(1, NCMAX):
                        score_chunk(pe, Unit(NT - 1, (NH - 1) // 3, (NH - 1) % 3), c)
                    for h in (NH - 2, NH - 1):
                        for j in range(2):
                            transpose_job(pe, Unit(NT - 1, h // 3, h % 3), j)
                    values_group(pe, Unit(NT - 1, (NH - 1) // 3, 0))
                    turn_back(pe, NT - 1)
                    if not full:
                        pe.wait_ge(t_step, worst_steps)
                        nc.tensor.transpose(t_ps[0:1, 1, 0:P], worst_row[:], ident[:]).then_inc(worst_ready, 1)

                @block.scalar
                def _(act):
                    def exponential(u, c):
                        k0, k1 = chunk_keys(u.i, c)
                        b = u.place(c)
                        if full:
                            act.wait_ge(max_ready, u.chunk(c) + 1)
                        elif c == 0:
                            act.wait_ge(max_ready, u.units() + 1)
                        else:
                            act.wait_ge(older_ready, u.older(c) + 1)
                        par = u.i % 2
                        cm = c if full else 0
                        dst = src = s_ps[:, b, 0:k1 - k0]
                        if c == 0:
                            old = u.back(RING)
                            if old is not None:
                                act.wait_ge(job_ready, old.all_jobs() + len(old.jobs))
                            dst = probs[:, u.buf, 0:k1 - k0]
                        nc.scalar.activation(dst, src, ACT.Exp, bias=negmax[:, par, u.h, cm:cm + 1], scale=-1.0,
                                             accum_out=sums[:, par, u.h, c:c + 1]).then_inc(exp_done, 1)

                    def weights(i):
                        act.wait_ge(spread_ready, i + 1 - first_multi)
                        n = chunks(i)
                        nc.scalar.activation(weight[:, :, 0:n], spread[:, :, 0:n], ACT.Exp).then_inc(weight_ready, 1)

                    def body(u, peeled):
                        for c in range(u.nc):
                            exponential(u, c)
                        if full and peeled == 0 and u.i > 0 and chunks(u.i - 1) > 1:
                            weights(u.i - 1)

                    for i in range(NT):
                        tile_units(act, i, body, not full)
                    if full:
                        weights(NT - 1)

                @block.gpsimd
                def _(pool):
                    nc.gpsimd.memset(vstage0[:], 0.0).then_inc(zeroed, 1)
                    nc.gpsimd.memset(vstage[:], 0.0).then_inc(zeroed, 1)
                    pool.wait_ge(zeroed, 2)

                    def stage(i, q, heads):
                        nb = blocks(i)
                        kt = i + 1 - nb
                        vs, h = (vstage0, 0) if heads == 1 else (vstage, q * 3 + 1)
                        done = 0
                        while done < nb:
                            r = (kt + done) % VR
                            n = min(nb - done, VR - r)
                            src = vals[:, r:r + n, bass.ds(h * HD, heads * HD)].rearrange("p b (j d) -> p b j d", d=HD)
                            last = nc.gpsimd.tensor_copy(vs[:, done:done + n, :, 0:HD], src)
                            done += n
                        last.then_inc(staged, 1)

                    def last_group(i):
                        pool.wait_ge(group_done, GROUPS * i + GROUPS - 1)
                        stage(i, GROUPS - 2, 3)

                    def body(u, peeled):
                        if peeled == 0 and u.i > 0:
                            last_group(u.i - 1)
                        if peeled == 1:
                            if u.i % 2 == 0:
                                pool.wait_ge(vals_loaded[(u.i // 2) % 2], 16 * (u.i // 4 + 1))
                            stage(u.i, 0, 1)
                        if peeled is None and u.s == 1:
                            k = u.q - 1
                            pool.wait_ge(group_done, k + (GROUPS * u.i + 1))
                            stage(u.i, k, 3)

                    for i in range(NT):
                        tile_units(pool, i, body, not full)
                    last_group(NT - 1)

                tsteps = [0]

                @block.vector
                def _(dve):
                    dve.wait_ge(decay_loaded, 16)

                    def serial(ins):
                        tsteps[0] += 1
                        ins.then_inc(t_step, 1)
                        dve.wait_ge(t_step, tsteps[0])

                    def evacuate(u, j):
                        if u is None or j >= len(u.jobs):
                            return
                        if j == 0:
                            need = u.groups_before_reuse()
                            if not isinstance(need, int) or need > 0:
                                dve.wait_ge(group_done, need)
                        dve.wait_ge(job_ready, u.all_jobs() + (j + 1))
                        b0, b1 = u.jobs[j]
                        src = t_ps[:, j, 0:P * (b1 - b0)].rearrange("p (b q) -> p b q", q=P)
                        d0 = WIN - blocks(u.i) + b0
                        nc.vector.tensor_tensor(probsT[:, u.slot(), b0:b1, :], src, dec_c[:, d0:d0 + b1 - b0, :],
                                                ALU.mult).then_inc(job_out, 1)

                    def maximum(u, c):
                        k0, k1 = chunk_keys(u.i, c)
                        b = u.place(c)
                        if c == 0:
                            dve.wait_ge(head_ready, u.units() + 1)
                        else:
                            dve.wait_ge(older_ready, u.older(c) + 1)
                        lo = 0 if full else max(0, k1 - k0 - P * WIN)
                        nc.vector.tensor_reduce(out=negmax[:, u.i % 2, u.h, c:c + 1], in_=s_ps[:, b, lo:k1 - k0],
                                                axis=AX_X, op=ALU.min).then_inc(max_ready, 1)

                    if not full:
                        serial(nc.vector.memset(worst[:], 0.0))

                    def spreads(i):
                        n = chunks(i)
                        dve.wait_ge(max_ready, chunk_base[i + 1])
                        if i > first_multi:
                            dve.wait_ge(weight_ready, i - first_multi)
                        serial(nc.vector.tensor_reduce(out=negtop[:], in_=negmax[:, i % 2, :, 0:n], axis=AX_X, op=ALU.min))
                        nc.vector.tensor_tensor(spread[:, :, 0:n], negtop[:].unsqueeze(2).to_broadcast([P, NH, n]),
                                                negmax[:, i % 2, :, 0:n], ALU.subtract).then_inc(spread_ready, 1)

                    def factors(i):
                        n = chunks(i)
                        dve.wait_ge(exp_done, chunk_base[i + 1])
                        if not full:
                            serial(nc.vector.reduce_sum(total[:], sums[:, i % 2, :, 0:n], axis=AX_X))
                            serial(nc.vector.tensor_tensor(worst[:], worst[:], total[:], ALU.max))
                            serial(nc.vector.reciprocal(factor[:], total[:]))
                            return
                        if n == 1:
                            serial(nc.vector.reciprocal(factor[:], sums[:, i % 2, :, 0]))
                            return
                        dve.wait_ge(weight_ready, i + 1 - first_multi)
                        serial(nc.vector.tensor_tensor(scaled[:, :, 0:n], weight[:, :, 0:n], sums[:, i % 2, :, 0:n], ALU.mult))
                        serial(nc.vector.reduce_sum(total[:], scaled[:, :, 0:n], axis=AX_X))
                        serial(nc.vector.reciprocal(total[:], total[:]))
                        serial(nc.vector.tensor_tensor(factor[:], total[:], weight[:, :, 0], ALU.mult))

                    def finish(i):
                        dve.wait_ge(back_ready, i + 1)
                        if i >= 2:
                            dve.wait_ge(y_stored[i % 2], 16 * (i // 2))
                        nc.vector.tensor_tensor(y_sb[:, i % 2, :].rearrange("p (h d) -> p h d", d=HD),
                                                t_ps[:, 0, :].rearrange("p (h w) -> p h w", w=TC)[:, :, 0:HD],
                                                factor[:].unsqueeze(2).to_broadcast([P, NH, HD]), ALU.mult).then_inc(y_out, 1)

                    def group_to_sb(u):
                        n = u.q + u.i * GROUPS
                        dve.wait_ge(group_done, n + 1)
                        if u.i > 0 and isinstance(u.h, int) and u.h == 0:
                            dve.wait_ge(back_ready, u.i)
                        w = TC * len(group_heads(u))
                        nc.vector.tensor_copy(yT_sb[0:w, u.q, :], g_ps[0:w, 0:P]).then_inc(group_out, 1)

                    def body(u, peeled):
                        t = u.back(TLAG)
                        prev = u.back(1)
                        older = list(range(1, prev.nc)) if full and prev is not None else []
                        for c in older[0:1]:
                            maximum(prev, c)
                        if not full and not pulls(prev):
                            maximum(u, 0)
                        if pulls(u):
                            maximum(following(u), 0)
                        if peeled == 2 and u.i > 0:
                            group_to_sb(Unit(u.i - 1, (NH - 1) // 3, 0))
                        if peeled == 3:
                            if u.i > 0:
                                finish(u.i - 1)
                            group_to_sb(Unit(u.i, 0, 0))
                        if peeled is None and u.s == 0:
                            group_to_sb(u.back(3))
                        evacuate(t, 0)
                        for c in older[1:2]:
                            maximum(prev, c)
                        evacuate(t, 1)
                        for c in older[2:]:
                            maximum(prev, c)
                        if full:
                            maximum(u, 0)
                        if u.i > 0:
                            if full and peeled == 0 and chunks(u.i - 1) > 1:
                                spreads(u.i - 1)
                            if peeled == 1:
                                factors(u.i - 1)

                    for i in range(NT):
                        tile_units(dve, i, body, not full)
                    end = Unit(NT - 1, NH // 3, NH % 3)
                    for c in range(1, NCMAX if full else 1):
                        maximum(end.back(1), c)
                    for lag in range(TLAG, 0, -1):
                        for j in range(2):
                            evacuate(end.back(lag), j)
                    group_to_sb(Unit(NT - 1, (NH - 1) // 3, 0))
                    if full:
                        spreads(NT - 1)
                    factors(NT - 1)
                    finish(NT - 1)
                    if not full:
                        serial(nc.vector.tensor_reduce(out=worst_row[:], in_=worst[:], axis=AX_X, op=ALU.max))
                        nc.vector.wait_ge(worst_ready, 1)
                        serial(nc.vector.tensor_reduce(out=worst_row[0:1, :], in_=t_ps[0:1, 1, 0:P], axis=AX_X, op=ALU.max))
                        serial(nc.vector.tensor_scalar(redo[:], worst_row[0:1, :], SUM_LIMIT, None, ALU.is_gt))


        attention(False)
        again = nc.values_load(redo[0:1, 0:1], min_val=0, max_val=1)
        with nc.If(again > 0):
            attention(True)

        B3 = 2
        NB = NT // B3
        y_loaded = [sem(f"y_loaded{b}") for b in range(2)]
        xr_loaded = [sem(f"xr_loaded{b}") for b in range(2)]
        yT_ready = sem("yT_ready")
        yT_out = sem("yT_out")
        att_ready = sem("att_ready")
        x2_done = sem("x2_done")
        raw_done = sem("raw_done")
        var_ready = sem("var_ready")
        dev_ready = sem("dev_ready")
        inv_done = sem("inv_done")
        n_ready = sem("n_ready")
        nT_ready = sem("nT_ready")
        nT_out = sem("nT_out")
        ff_ready = sem("ff_ready")
        biased = sem("biased")
        o_ready = sem("o_ready")
        o_stored = [sem(f"o_stored{b}") for b in range(2)]

        s3 = ExitStack()
        with s3:
            x_sb = sb("x_sb", [P, 2, B3, C], fp32, s3)
            yy = sb("yy", [P, 2, B3, C], fp32, s3)
            yT = sb("yT", [P, 2, B3, CH, P], fp32, s3)
            x2 = sb("x2", [P, 2, B3, C], fp32, s3)
            x2b = sb("x2b", [P, 2, B3, C], fp32, s3)
            nrm = sb("nrm", [P, 2, B3, C], fp32, s3)
            nT = sb("nT", [P, 2, B3, CH, P], fp32, s3)
            o_sb = sb("o_sb", [P, 2, B3, C], fp32, s3)
            q6 = sb("q6", [P, B3, 6], fp32, s3)
            mv3 = sb("mv3", [P, 2, B3, 2], fp32, s3)
            sd3 = sb("sd3", [P, 2, B3], fp32, s3)
            rs3 = sb("rs3", [P, 2, B3], fp32, s3)
            yT_ps = s3.enter_context(nc.psum_tensor("yT_ps", [P, 2, B3, CH, P], fp32))
            at_ps = s3.enter_context(nc.psum_tensor("at_ps", [P, 2, B3, C], fp32))
            nT_ps = s3.enter_context(nc.psum_tensor("nT_ps", [P, 2, B3, CH, P], fp32))
            ff_ps = s3.enter_context(nc.psum_tensor("ff_ps", [P, 2, B3, C], fp32))
            block = s3.enter_context(nc.Block())

            DEPTH = 3
            HEAD = DEPTH + 1

            def pipeline(eng, body):
                def peeled_at(s):
                    return lambda lag: (s - lag, (s - lag) % 2, (s - lag) // 2, True) if 0 <= s - lag < NB else None

                def loop_at(k, r):
                    return lambda lag: (k * 2 + (r - lag), (r - lag) % 2, k + (r - lag) // 2, False)

                for s in range(HEAD):
                    body(peeled_at(s))
                with eng.Fori(HEAD // 2, NB // 2) as k:
                    for r in range(2):
                        body(loop_at(k, r))
                for s in range(NB, NB + DEPTH):
                    body(peeled_at(s))

            def reused(batch):
                return not batch[3] or batch[0] >= 2

            @block.sync
            def _(sp):
                def load(src, dst, sem_, m):
                    sp.dma_start(dst[:, m % 2], src[:, B3 * m:B3 * (m + 1), :]).then_inc(sem_[m % 2], 16)

                for m in (0, 1):
                    load(y_tiles, yy, y_loaded, m)
                    load(x_tiles, x_sb, xr_loaded, m)
                for s in range(NB + DEPTH):
                    if s + 2 < NB:
                        sp.wait_ge(yT_ready, s + 1)
                        load(y_tiles, yy, y_loaded, s + 2)
                    if 1 <= s and s + 1 < NB:
                        sp.wait_ge(x2_done, s)
                        load(x_tiles, x_sb, xr_loaded, s + 1)
                    m = s - DEPTH
                    if m >= 0:
                        sp.wait_ge(o_ready, m + 1)
                        sp.dma_start(out_tiles[:, B3 * m:B3 * (m + 1), :], o_sb[:, m % 2]).then_inc(o_stored[m % 2], 16)
                for b in range(2):
                    sp.wait_ge(o_stored[b], 16 * (NB // 2))

            @block.tensor
            def _(pe):
                def project(batch):
                    m, b, _, _ = batch
                    pe.wait_ge(yT_out, m + 1)
                    if reused(batch):
                        pe.wait_ge(x2_done, m - 1)
                    for t in range(B3):
                        for cc in range(CH):
                            last = nc.tensor.matmul(at_ps[:, b, t, :], yT[:, b, t, cc, :], wp_g[:, cc, :],
                                                    start=(cc == 0), stop=(cc == CH - 1))
                    last.then_inc(att_ready, 1)

                def transpose_y(batch):
                    m, b, half, _ = batch
                    pe.wait_ge(y_loaded[b], (half + 1) * 16)
                    if reused(batch):
                        pe.wait_ge(yT_out, m - 1)
                    for t in range(B3):
                        for cc in range(CH):
                            last = nc.tensor.transpose(yT_ps[:, b, t, cc, :], yy[:, b, t, P * cc:P * (cc + 1)], ident[:])
                    last.then_inc(yT_ready, 1)

                def linear(batch):
                    m, b, _, _ = batch
                    pe.wait_ge(nT_out, m + 1)
                    if reused(batch):
                        pe.wait_ge(o_ready, m - 1)
                    for t in range(B3):
                        for cc in range(CH):
                            last = nc.tensor.matmul(ff_ps[:, b, t, :], nT[:, b, t, cc, :], wf_g[:, cc, :],
                                                    start=(cc == 0), stop=(cc == CH - 1))
                    last.then_inc(ff_ready, 1)

                def transpose_n(batch):
                    m, b, _, _ = batch
                    pe.wait_ge(n_ready, m + 1)
                    if reused(batch):
                        pe.wait_ge(nT_out, m - 1)
                    for t in range(B3):
                        for cc in range(CH):
                            last = nc.tensor.transpose(nT_ps[:, b, t, cc, :], nrm[:, b, t, P * cc:P * (cc + 1)], ident[:])
                    last.then_inc(nT_ready, 1)

                def body(at):
                    for work, lag in ((project, 1), (transpose_y, 0), (linear, 3), (transpose_n, 2)):
                        if at(lag) is not None:
                            work(at(lag))

                pipeline(pe, body)

            @block.scalar
            def _(act):
                def copy_y(batch):
                    m, b, _, _ = batch
                    act.wait_ge(yT_ready, m + 1)
                    if reused(batch):
                        act.wait_ge(att_ready, m - 1)
                    nc.scalar.copy(yT[:, b], yT_ps[:, b]).then_inc(yT_out, 1)

                def deviation(batch):
                    m, b, _, _ = batch
                    act.wait_ge(var_ready, m + 1)
                    if reused(batch):
                        act.wait_ge(inv_done, m - 1)
                    nc.scalar.activation(sd3[:, b, :], mv3[:, b, :, 1], ACT.Sqrt, bias=eps_t[:, 0:1]).then_inc(dev_ready, 1)

                def copy_n(batch):
                    m, b, _, _ = batch
                    act.wait_ge(nT_ready, m + 1)
                    if reused(batch):
                        act.wait_ge(ff_ready, m - 1)
                    nc.scalar.copy(nT[:, b], nT_ps[:, b]).then_inc(nT_out, 1)

                def body(at):
                    for work, lag in ((copy_y, 0), (deviation, 1), (copy_n, 2)):
                        if at(lag) is not None:
                            work(at(lag))

                pipeline(act, body)

            @block.gpsimd
            def _(pool):
                def add_bias(batch):
                    m, b, _, _ = batch
                    pool.wait_ge(x2_done, m + 1)
                    if reused(batch):
                        pool.wait_ge(o_ready, m - 1)
                    nc.gpsimd.tensor_tensor(x2b[:, b], x2[:, b], f_bias[:].unsqueeze(1).to_broadcast([P, B3, C]),
                                            ALU.add).then_inc(biased, 1)

                def body(at):
                    if at(1) is not None:
                        add_bias(at(1))

                pipeline(pool, body)

            @block.vector
            def _(dve):
                def residual(batch):
                    m, b, half, _ = batch
                    dve.wait_ge(att_ready, m + 1)
                    dve.wait_ge(xr_loaded[b], (half + 1) * 16)
                    if reused(batch):
                        dve.wait_ge(biased, m - 1)
                    nc.vector.tensor_tensor(x2[:, b], x_sb[:, b], at_ps[:, b], ALU.add).then_inc(x2_done, 1)
                    dve.wait_ge(x2_done, m + 1)
                    for t in range(B3):
                        last = nc.vector.bn_stats(q6[:, t, :], x2[:, b, t, :])
                    last.then_inc(raw_done, 1)
                    dve.wait_ge(raw_done, m + 1)

                def result(batch):
                    m, b, half, _ = batch
                    dve.wait_ge(ff_ready, m + 1)
                    dve.wait_ge(biased, m + 1)
                    if reused(batch):
                        dve.wait_ge(o_stored[b], half * 16)
                    nc.vector.tensor_tensor(o_sb[:, b], ff_ps[:, b], x2b[:, b], ALU.add).then_inc(o_ready, 1)

                def means(batch):
                    m, b, _, _ = batch
                    for t in range(B3):
                        last = nc.vector.bn_aggr(mv3[:, b, t, :], q6[:, t, :])
                    last.then_inc(var_ready, 1)

                def normalise(batch):
                    m, b, _, _ = batch
                    dve.wait_ge(dev_ready, m + 1)
                    nc.vector.reciprocal(rs3[:, b, :], sd3[:, b, :]).then_inc(inv_done, 1)
                    dve.wait_ge(inv_done, m + 1)
                    if reused(batch):
                        dve.wait_ge(nT_ready, m - 1)
                    dve.wait_ge(var_ready, m + 1)
                    for t in range(B3):
                        last = nc.vector.tensor_scalar(nrm[:, b, t, :], x2[:, b, t, :], mv3[:, b, t, 0:1], rs3[:, b, t:t + 1],
                                                       ALU.subtract, ALU.mult)
                    last.then_inc(n_ready, 1)

                def body(at):
                    for work, lag in ((residual, 1), (result, 3), (means, 1), (normalise, 1)):
                        if at(lag) is not None:
                            work(at(lag))

                pipeline(dve, body)


def kernel(**inputs):
    import numpy as _np
    import concourse.bacc as _bacc
    from concourse import mybir as _mybir
    from concourse.bass_utils import run_bass_kernel_spmd as _run

    def a(name):
        return _np.asarray(inputs[name])

    P, WIN, LENGTH, ECHOIC = 128, 5, 512, 16
    ramp = _np.linspace(0.0, 1.0, LENGTH - ECHOIC + 1).astype(_np.float32)
    decay = 1.0 - _np.power(ramp, _np.float32(1.0 / _np.e))
    decay = _np.concatenate([_np.ones(ECHOIC - 1), decay]).astype(_np.float32)
    dist = _np.arange(P)[:, None] + P * (WIN - 1) - _np.arange(P * WIN)[None, :]
    rows = _np.where((dist >= 0) & (dist < LENGTH), decay[_np.clip(dist, 0, LENGTH - 1)], 0).astype(_np.float32)
    cols = rows.reshape(P, WIN, P).transpose(2, 1, 0)
    bf16 = _mybir.dt.np(_mybir.dt.bfloat16)
    causal = _np.where(_np.arange(P)[None, :] > _np.arange(P)[:, None], 1e30, 0.0).astype(bf16)

    ins = {
        "x": a("L0_attn_x")[0],
        "w_attn": a("L0_attn_W_attn"), "w_proj": a("L0_attn_W_proj"),
        "ffn_wT": a("L0_ffn_W").T, "ffn_b": a("L0_ffn_b")[None, :],
        "lora_downT": a("L0_ffn_lora_down").T, "lora_upT": a("L0_ffn_lora_up").T,
        "down_aux": a("L0_ffn_down_aux"), "up_auxT": a("L0_ffn_up_aux").T,
        "cond_cols": a("L0_c").reshape(2, P).T, "w_mod": a("L0_wmod"),
        "ident_in": _np.eye(P, dtype=_np.float32), "causal_in": causal, "decay_cols": cols,
    }
    nc = _bacc.Bacc("TRN2", target_bir_lowering=False, num_devices=1)
    arrays, args = {}, []
    for name, v in ins.items():
        v = _np.ascontiguousarray(v)
        arrays[f"{name}_dram"] = v
        args.append(nc.dram_tensor(f"{name}_dram", v.shape, _mybir.dt.from_np(v.dtype), kind="ExternalInput").ap())
    out = nc.dram_tensor("out_dram", ins["x"].shape, _mybir.dt.float32, kind="ExternalOutput").ap()
    bass_adaln_block_kernel(nc, *args, out)
    r = _run(nc, [arrays], core_ids=[0])
    return r.results[0]["out_dram"][None]
```
